# Optimizing a Trainium2 kernel written in Bass

```python
import numpy as np
import jax
import jax.numpy as jnp

def _softmax(x, axis=-1):
    return jax.nn.softmax(x, axis=axis)

def _gelu(x):
    return jax.nn.gelu(x, approximate=True)

def _silu(x):
    return jax.nn.silu(x)

def _sigmoid(x):
    return jax.nn.sigmoid(x)

def _layernorm(x, axis=-1, eps=1e-05):
    m = jnp.mean(x, axis=axis, keepdims=True)
    v = jnp.var(x, axis=axis, keepdims=True)
    return (x - m) / jnp.sqrt(v + eps)

def _scatter_add(tgt, idx, src, axis=0):
    return tgt.at[idx].add(src)

def _segment_sum(src, seg, n):
    return jax.ops.segment_sum(src, seg, n)
kernel_name = 'mk_cond_resid_d1_seqx_r8_198ce9'

def setup_inputs(seed: int=0):
    np.random.seed(seed)
    _w = jnp.asarray

    def _rec_inputs():
        import jax
        import jax.numpy as jnp
        _rk = jax.random.key(seed)
        x = 7.22e-05 + 1 * jax.random.normal(jax.random.fold_in(_rk, 1), (32, 128, 128), jnp.float32)
        _lenS = 128 - jax.random.randint(jax.random.fold_in(_rk, 7), (32,), 0, max(1, 128 // 4) + 1, jnp.int32)
        _lenS2 = 128 - jax.random.randint(jax.random.fold_in(_rk, 8), (32,), 0, max(1, 128 // 4) + 1, jnp.int32)
        cond_8 = -0.104238 + 1.01173 * jax.random.normal(jax.random.fold_in(_rk, 11), (32, 8), jnp.float32)
        return (x, cond_8)
    x, cond_8 = _rec_inputs()

    def _L0_cond_setup():
        import jax, jax.numpy as jnp
        import numpy as np
        TOP_K = 2
        NUM_MOE_LAYERS = 12

        def _gemma_mlp(x, gate_w, up_w, down_w):
            g = jnp.einsum('bsh,hi->bsi', x, gate_w)
            u = jnp.einsum('bsh,hi->bsi', x, up_w)
            return jnp.einsum('bsi,ih->bsh', jax.nn.gelu(g, approximate=True) * u, down_w)
        key = jax.random.key(seed)
        ks = jax.random.split(key, 8)
        B, S, H, I, E = (32, 32, 128, 512, 8)
        std = 0.02
        return {'x': jax.random.normal(ks[0], (B, S, H), jnp.float32), 'router_logits': jax.random.normal(ks[1], (B, E), jnp.float32), 'skill_gate': jax.random.normal(ks[2], (E, H, I), jnp.float32) * std, 'skill_up': jax.random.normal(ks[3], (E, H, I), jnp.float32) * std, 'skill_down': jax.random.normal(ks[4], (E, I, H), jnp.float32) * std, 'shared_gate': jax.random.normal(ks[5], (H, I), jnp.float32) * std, 'shared_up': jax.random.normal(ks[6], (H, I), jnp.float32) * std, 'shared_down': jax.random.normal(ks[7], (I, H), jnp.float32) * std}
    _L0_cond_all = _L0_cond_setup()
    _L0_cond_in = {k: v for k, v in _L0_cond_all.items() if k in ('skill_gate', 'skill_up', 'skill_down', 'shared_gate', 'shared_up', 'shared_down')}
    del _L0_cond_all
    return {'x': x, 'cond_8': cond_8, 'L0_cond_skill_gate': _L0_cond_in['skill_gate'], 'L0_cond_skill_up': _L0_cond_in['skill_up'], 'L0_cond_skill_down': _L0_cond_in['skill_down'], 'L0_cond_shared_gate': _L0_cond_in['shared_gate'], 'L0_cond_shared_up': _L0_cond_in['shared_up'], 'L0_cond_shared_down': _L0_cond_in['shared_down']}

def reference(x, cond_8, L0_cond_skill_gate, L0_cond_skill_up, L0_cond_skill_down, L0_cond_shared_gate, L0_cond_shared_up, L0_cond_shared_down):
    import jax
    import jax.numpy as jnp

    def _L0_cond_ref(x, router_logits, skill_gate, skill_up, skill_down, shared_gate, shared_up, shared_down):
        import jax, jax.numpy as jnp
        import numpy as np
        TOP_K = 2
        NUM_MOE_LAYERS = 12

        def _gemma_mlp(x, gate_w, up_w, down_w):
            g = jnp.einsum('bsh,hi->bsi', x, gate_w)
            u = jnp.einsum('bsh,hi->bsi', x, up_w)
            return jnp.einsum('bsi,ih->bsh', jax.nn.gelu(g, approximate=True) * u, down_w)
        B = x.shape[0]
        E = skill_gate.shape[0]
        rw = jax.nn.softmax(router_logits.astype(jnp.float32), axis=-1)
        w, sel = jax.lax.top_k(rw, TOP_K)
        w = w / w.sum(axis=-1, keepdims=True)
        w = w.astype(x.dtype)
        scale = 1.0 / NUM_MOE_LAYERS
        w = scale * w + (1.0 - scale) * jax.lax.stop_gradient(w)
        dense_w = jnp.zeros((B, E), x.dtype).at[jnp.arange(B)[:, None], sel].add(w)

        def step(acc, params):
            g, u, d, we = params
            return (acc + we[:, None, None] * _gemma_mlp(x, g, u, d), None)
        out, _ = jax.lax.scan(step, jnp.zeros_like(x), (skill_gate, skill_up, skill_down, dense_w.T))
        out = out + _gemma_mlp(x, shared_gate, shared_up, shared_down)
        return out
    x = x + _L0_cond_ref(x, cond_8, L0_cond_skill_gate, L0_cond_skill_up, L0_cond_skill_down, L0_cond_shared_gate, L0_cond_shared_up, L0_cond_shared_down)
    return x

_drawn_inputs = setup_inputs


def setup_inputs(seed=0):
    import zlib

    import numpy as np

    out = dict(_drawn_inputs(seed))
    spreads = {}
    factors = {'cond_8': 7.115,
     'L0_cond_skill_gate': 6.409,
     'L0_cond_skill_up': 6.323,
     'L0_cond_skill_down': 6.326,
     'L0_cond_shared_gate': 4.734,
     'L0_cond_shared_up': 4.652,
     'L0_cond_shared_down': 4.649}
    for name, (base, spread) in spreads.items():
        noise = np.random.default_rng([zlib.crc32(name.encode()), seed]).standard_normal(out[name].shape)
        drawn = base * np.exp(spread * noise) if base else spread * noise
        out[name] = jnp.asarray(drawn.astype(out[name].dtype))
    for name, factor in factors.items():
        out[name] = (out[name] * factor).astype(out[name].dtype)
    return out
```

```python
from contextlib import ExitStack

import concourse.bass as bass
from concourse import mybir

ALU = mybir.AluOpType
ACT = mybir.ActivationFunctionType
AX = mybir.AxisListType
F32 = mybir.dt.float32
F16 = mybir.dt.float16
BF16 = mybir.dt.bfloat16
I32 = mybir.dt.int32
U32 = mybir.dt.uint32
RMAX = bass.bass_isa.ReduceOp.max

P = 128
TOP_K = 2
NUM_MOE_LAYERS = 12

EXP_SHIFT = 24
SCALE_FIELD = 204
INV_FIELD = 254 - SCALE_FIELD
ONE_EXP = float(2 ** 23)
HIDDEN_SHIFT = float(2.0 ** -45)


def build(nc, xT, cond, skills, shared, outT):
    B, E = cond.shape
    H = xT.shape[0]
    S = xT.shape[1] // B
    W = shared.shape[1]
    I = W // 3
    C = I // P
    GR = 512 // S
    G = B // GR
    GN = GR * S
    assert H == P and S == P and I == GN and C == 4 and G == 8 and E == 8
    SQ_GROUPS = 4
    EG = E // SQ_GROUPS
    GATE, UP, DOWN = 0, I, 2 * I

    ctx = ExitStack()
    with ctx:
        def sb(name, shape, dt):
            return ctx.enter_context(nc.sbuf_tensor(name, shape, dt))

        def ps(name, shape, dt=F32):
            return ctx.enter_context(nc.psum_tensor(name, shape, dt))

        def sem(name):
            return ctx.enter_context(nc.semaphore(name))

        acc = sb("acc", [P, B * S], F32)
        x_hi = sb("x_hi", [P, B * S], F16)
        x_lo = sb("x_lo", [P, B * S], F16)
        wsh32 = sb("wsh32", [P, W], F32)
        wsh_hi = sb("wsh_hi", [P, W], F16)
        wsh_lo = sb("wsh_lo", [P, W], F16)
        wsk32 = sb("wsk32", [P, E * W], F32)
        wsk_hi = sb("wsk_hi", [P, E * W], F16)
        wsk_lo = sb("wsk_lo", [P, E * W], F16)
        sq_x = sb("sq_x", [P, B * S], BF16)
        sq_sh = sb("sq_sh", [P, W], BF16)
        sq_sk = sb("sq_sk", [P, 2 * EG * W], BF16)
        ones_col = sb("ones_col", [P, 1], BF16)
        gel = sb("gel", [P, 2, GN], F32)
        h32 = sb("h32", [P, 3, GN], F32)
        h_hi = sb("h_hi", [P, 4, GN], F16)
        h_lo = sb("h_lo", [P, 4, GN], F16)
        NS = 3 + G + 3
        XC, KC = 3, 3 + G
        n_part = sb("n_part", [P, NS], F32)
        n_all = sb("n_all", [P, NS], F32)
        e_half = sb("e_half", [P, NS], U32)
        s_bits = sb("s_bits", [P, NS], I32)
        i_bits = sb("i_bits", [P, NS], I32)
        sc = s_bits[:, :].bitcast(F32)
        inv = i_bits[:, :].bitcast(F32)
        prod = sb("prod", [P, 4], F32)
        T = G * C + B * TOP_K
        gate_sc = sb("gate_sc", [P, T], F32)
        factor = sb("factor", [P, T], F32)
        sh_inv = sb("sh_inv", [P, G], F32)
        sk_inv = sb("sk_inv", [P, B], F32)
        tmp_g = sb("tmp_g", [P, 2, G], F32)
        tmp_k = sb("tmp_k", [P, 2, G], F32)
        logits = sb("logits", [B, E], F32)
        neg_max = sb("neg_max", [B, 1], F32)
        expv = sb("expv", [B, E], F32)
        expsum = sb("expsum", [B, 1], F32)
        rsum = sb("rsum", [B, 1], F32)
        probs = sb("probs", [B, E], F32)
        top_v = sb("top_v", [B, 8], F32)
        top_i = sb("top_i", [B, 8], U32)
        pair = sb("pair", [B, 1], F32)
        rpair = sb("rpair", [B, 1], F32)
        w_raw = sb("w_raw", [B, TOP_K], F32)
        w_live = sb("w_live", [B, TOP_K], F32)
        route = sb("route", [B, 2 * TOP_K], F32)
        ident = sb("ident", [B, B], F32)
        ones32 = sb("ones32", [B, P], F32)
        spread = sb("spread", [B, B, 2 * TOP_K], F32)
        wexp = sb("wexp", [P, B, TOP_K], F32)
        eoff = sb("eoff", [1, B * TOP_K], I32)

        g_ps = [ps(f"g_ps{k}", [P, GN]) for k in range(2)]
        u_ps = [ps(f"u_ps{k}", [P, GN]) for k in range(2)]
        sh_out = ps("sh_out", [P, GN])
        row_out = [ps(f"row_out{k}", [P, GN]) for k in range(2)]
        norm_w = ps("norm_w", [P, 512])
        NRM_X0, NRM_SH, NRM_SK = 0, GR, GR + 3 * C
        NRM = NRM_SK + E * 3 * C
        norm_x = row_out[0][:, 0:B - GR]
        routed = row_out[1][:, 0:2 * TOP_K * B].rearrange("p (b q) -> p b q", b=B)

        cond_in = sem("cond_in")
        x0_in = sem("x0_in")
        xr_in = sem("xr_in")
        sh_in = sem("sh_in")
        sk_in = [sem(f"sk_in{n}") for n in range(SQ_GROUPS)]
        zeroed = sem("zeroed")
        consts = sem("consts")
        r_negmax = sem("r_negmax")
        r_exp = sem("r_exp")
        r_step = sem("r_step")
        r_spread = sem("r_spread")
        r_routed = sem("r_routed")
        r_table = sem("r_table")
        sq_act = sem("sq_act")
        sq_pool = sem("sq_pool")
        norms = sem("norms")
        n_max = sem("n_max")
        n_red = sem("n_red")
        s_step = sem("s_step")
        scaled = sem("scaled")
        tab_sh = sem("tab_sh")
        tab_sk = sem("tab_sk")
        t_step = sem("t_step")
        x_hi_ok = sem("x_hi_ok")
        x_lo_ok = sem("x_lo_ok")
        sh_hi_ok = sem("sh_hi_ok")
        sh_lo_ok = sem("sh_lo_ok")
        sk_hi_ok = sem("sk_hi_ok")
        sk_lo_ok = sem("sk_lo_ok")
        gu_ready = sem("gu_ready")
        gelu_ready = sem("gelu_ready")
        h_ready = sem("h_ready")
        hi_ready = sem("hi_ready")
        lo_ready = sem("lo_ready")
        down_done = sem("down_done")
        added = sem("added")
        stored = sem("stored")

        SH_STEPS = G * C

        block = ctx.enter_context(nc.Block())

        @block.sync
        def _(sp):
            sp.dma_start(logits[:, :], cond).then_inc(cond_in, 16)
            sp.dma_start(acc[:, 0:GN], xT[:, 0:GN]).then_inc(x0_in, 16)
            sp.dma_start(wsh32[:, :], shared).then_inc(sh_in, 16)
            sp.dma_start(acc[:, GN:], xT[:, GN:]).then_inc(xr_in, 16)
            for n in range(SQ_GROUPS):
                sp.dma_start(wsk32[:, n * EG * W:(n + 1) * EG * W], skills[:, n * EG * W:(n + 1) * EG * W]).then_inc(sk_in[n], 16)
            with sp.Fori(0, G) as j:
                sp.wait_ge(added, GR * j + (G + GR))
                sp.dma_start(outT[:, bass.ds(j * GN, GN)], acc[:, bass.ds(j * GN, GN)]).then_inc(stored, 16)
            sp.wait_ge(stored, 16 * G)

        @block.gpsimd
        def _(pool):
            nc.gpsimd.memset(ones_col[:, :], 1.0).then_inc(consts, 1)
            nc.gpsimd.memset(ones32[:, :], 1.0).then_inc(consts, 1)
            nc.gpsimd.memset(ident[:, :], 0.0).then_inc(zeroed, 1)
            pool.wait_ge(zeroed, 1)
            nc.gpsimd.affine_select(out=ident[:, :], in_=ident[:, :], compare_op=ALU.not_equal, fill=1.0, base=0,
                                    pattern=[[-1, B]], channel_multiplier=1).then_inc(consts, 1)

            def reduce_norms(batch, a, b):
                pool.wait_ge(n_max, batch + 1)
                nc.gpsimd.partition_all_reduce(n_all[:, a:b], n_part[:, a:b], P, RMAX).then_inc(n_red, 1)

            def square(n):
                pool.wait_ge(sk_in[n], 16)
                if n >= 2:
                    pool.wait_ge(norms, 2 + n - 1)
                w = wsk32[:, n * EG * W:(n + 1) * EG * W]
                o = (n % 2) * EG * W
                nc.gpsimd.tensor_tensor(sq_sk[:, o:o + EG * W], w, w, ALU.mult).then_inc(sq_pool, 1)

            def low_part(t, k3, k4):
                pool.wait_ge(hi_ready, t + 1)
                nc.gpsimd.tensor_tensor(h_lo[:, k4, :], h32[:, k3, :], h_hi[:, k4, :], ALU.subtract).then_inc(lo_ready, 1)

            reduce_norms(0, 0, XC + 1)
            reduce_norms(1, XC + 1, KC)
            square(0)
            for t in range(SH_STEPS):
                low_part(t, t % 3, t % 4)
                if t % C == C - 1 and 0 < t // C < SQ_GROUPS:
                    square(t // C)
                if t == C * SQ_GROUPS:
                    reduce_norms(2, KC, NS)
            with pool.Fori(0, (B * TOP_K - 4) // 12) as i:
                for s in range(12):
                    low_part(SH_STEPS + 12 * i + s, (SH_STEPS + s) % 3, s % 4)
            for t in range(B * TOP_K - 4, B * TOP_K):
                low_part(SH_STEPS + t, (SH_STEPS + t) % 3, t % 4)

        @block.scalar
        def _(act):
            act.wait_ge(r_negmax, 1)
            act.wait_ge(cond_in, 16)
            nc.scalar.activation(expv[:, :], logits[:, :], ACT.Exp, bias=neg_max[:, 0:1],
                                 accum_out=expsum[:, :]).then_inc(r_exp, 1)
            act.wait_ge(x0_in, 16)
            nc.scalar.activation(sq_x[:, 0:GN], acc[:, 0:GN], ACT.Square).then_inc(sq_act, 1)
            act.wait_ge(sh_in, 16)
            nc.scalar.activation(sq_sh[:, :], wsh32[:, :], ACT.Square).then_inc(sq_act, 1)
            act.wait_ge(xr_in, 16)
            nc.scalar.activation(sq_x[:, GN:], acc[:, GN:], ACT.Square).then_inc(sq_act, 1)

            def x_high(j):
                nc.scalar.activation(x_hi[:, bass.ds(j * GN, GN)], acc[:, bass.ds(j * GN, GN)], ACT.Copy,
                                     scale=sc[:, bass.ds(XC + j, 1)]).then_inc(x_hi_ok, 1)

            def gelu(t, k, table, n):
                act.wait_ge(gu_ready, t + 1)
                act.wait_ge(table, n)
                nc.scalar.activation(gel[:, k, :], g_ps[k][:, :], ACT.Gelu_apprx_tanh,
                                     scale=gate_sc[:, bass.ds(t, 1)]).then_inc(gelu_ready, 1)

            act.wait_ge(scaled, 1)
            x_high(0)
            for q in range(3):
                nc.scalar.activation(wsh_hi[:, q * I:(q + 1) * I], wsh32[:, q * I:(q + 1) * I], ACT.Copy,
                                     scale=sc[:, q:q + 1]).then_inc(sh_hi_ok, 1)
            act.wait_ge(scaled, 2)
            for c in range(C):
                gelu(c, c % 2, tab_sh, 1)
                x_high(1 + c)
            with act.Fori(1, SQ_GROUPS) as j:
                for c in range(C):
                    gelu(j * C + c, c % 2, tab_sh, 2)
                x_high(j + C)
            with act.Fori(SQ_GROUPS, G) as j:
                for c in range(C):
                    gelu(j * C + c, c % 2, tab_sh, 2)
                    if c < 3:
                        act.wait_ge(scaled, 3)
                        o = (j - SQ_GROUPS) * (EG * W)
                        hi = wsk_hi[:, bass.ds(o, EG * W)].rearrange("p (e w) -> p e w", e=EG)
                        w = wsk32[:, bass.ds(o, EG * W)].rearrange("p (e w) -> p e w", e=EG)
                        nc.scalar.activation(hi[:, :, c * I:(c + 1) * I], w[:, :, c * I:(c + 1) * I], ACT.Copy,
                                             scale=sc[:, KC + c:KC + c + 1]).then_inc(sk_hi_ok, 1)
            with act.Fori(0, B) as b:
                for k in range(TOP_K):
                    gelu(b * TOP_K + (SH_STEPS + k), k, tab_sk, 1)

        @block.vector
        def _(dve):
            dve.wait_ge(cond_in, 16)
            nc.vector.tensor_reduce(neg_max[:, :], logits[:, :], AX.X, ALU.max, negate=True).then_inc(r_negmax, 1)
            dve.wait_ge(r_exp, 1)
            nc.vector.reciprocal(rsum[:, :], expsum[:, :]).then_inc(r_step, 1)
            dve.wait_ge(r_step, 1)
            nc.vector.tensor_scalar(probs[:, :], expv[:, :], rsum[:, 0:1], None, ALU.mult).then_inc(r_step, 1)
            dve.wait_ge(r_step, 2)
            nc.vector.max(top_v[:, :], probs[:, :]).then_inc(r_step, 1)
            dve.wait_ge(r_step, 3)
            nc.vector.max_index(top_i[:, :], top_v[:, :], probs[:, :]).then_inc(r_step, 1)
            nc.vector.tensor_tensor(pair[:, :], top_v[:, 0:1], top_v[:, 1:2], ALU.add).then_inc(r_step, 1)
            dve.wait_ge(r_step, 5)
            nc.vector.tensor_copy(route[:, TOP_K:], top_i[:, 0:TOP_K]).then_inc(r_step, 1)
            nc.vector.reciprocal(rpair[:, :], pair[:, :]).then_inc(r_step, 1)
            dve.wait_ge(r_step, 7)
            nc.vector.tensor_scalar(w_raw[:, :], top_v[:, 0:TOP_K], rpair[:, 0:1], None, ALU.mult).then_inc(r_step, 1)
            dve.wait_ge(r_step, 8)
            nc.vector.tensor_scalar(w_live[:, :], w_raw[:, :], 1.0 / NUM_MOE_LAYERS, None, ALU.mult).then_inc(r_step, 1)
            dve.wait_ge(r_step, 9)
            nc.vector.scalar_tensor_tensor(out=route[:, 0:TOP_K], in0=w_raw[:, :], scalar=1.0 - 1.0 / NUM_MOE_LAYERS,
                                           in1=w_live[:, :], op0=ALU.mult, op1=ALU.add).then_inc(r_step, 1)
            dve.wait_ge(r_step, 10)
            dve.wait_ge(consts, 3)
            for q in range(2 * TOP_K):
                nc.vector.tensor_scalar(spread[:, :, q], ident[:, :], route[:, q:q + 1], None, ALU.mult).then_inc(r_spread, 1)

            def scales(batch, a, b):
                dve.wait_ge(n_red, batch + 1)
                nc.vector.tensor_scalar(e_half[:, a:b], n_all[:, a:b].bitcast(U32), EXP_SHIFT, None,
                                        ALU.logical_shift_right).then_inc(s_step, 1)
                dve.wait_ge(s_step, batch + 1)
                nc.vector.tensor_scalar(i_bits[:, a:b], e_half[:, a:b], ONE_EXP, INV_FIELD * ONE_EXP,
                                        ALU.mult, ALU.add)
                nc.vector.tensor_scalar(s_bits[:, a:b], e_half[:, a:b], -ONE_EXP, SCALE_FIELD * ONE_EXP,
                                        ALU.mult, ALU.add).then_inc(scaled, 1)
                dve.wait_ge(scaled, batch + 1)

            def x_low(j):
                dve.wait_ge(x_hi_ok, j + 1)
                nc.vector.scalar_tensor_tensor(out=x_lo[:, bass.ds(j * GN, GN)], in0=acc[:, bass.ds(j * GN, GN)],
                                               scalar=sc[:, bass.ds(XC + j, 1)], in1=x_hi[:, bass.ds(j * GN, GN)],
                                               op0=ALU.mult, op1=ALU.subtract).then_inc(x_lo_ok, 1)

            def shared_tables(n, a, b):
                ix, sx = inv[:, XC + a:XC + b], sc[:, XC + a:XC + b]
                n_g = b - a
                nc.vector.tensor_scalar(gate_sc[:, a * C:b * C].rearrange("p (j c) -> p j c", c=C),
                                        ix.unsqueeze(2).broadcast_to([P, n_g, C]), inv[:, 0:1], None, ALU.mult).then_inc(t_step, 1)
                nc.vector.tensor_scalar(factor[:, a * C:b * C].rearrange("p (j c) -> p j c", c=C),
                                        sx.unsqueeze(2).broadcast_to([P, n_g, C]), HIDDEN_SHIFT, sc[:, 0:1],
                                        ALU.mult, ALU.mult).then_inc(t_step, 1)
                nc.vector.tensor_scalar(tmp_g[:, 0, a:b], ix, inv[:, 1:2], 1.0 / HIDDEN_SHIFT,
                                        ALU.mult, ALU.mult).then_inc(t_step, 1)
                dve.wait_ge(t_step, 4 * n + 3)
                nc.vector.tensor_scalar(tmp_g[:, 1, a:b], tmp_g[:, 0, a:b], inv[:, 2:3], None, ALU.mult).then_inc(t_step, 1)
                dve.wait_ge(t_step, 4 * n + 4)
                nc.vector.tensor_tensor(sh_inv[:, a:b], tmp_g[:, 1, a:b], gate_sc[:, a * C:b * C:C], ALU.mult).then_inc(tab_sh, 1)

            def hidden(t, kp, k3, k4):
                dve.wait_ge(gelu_ready, t + 1)
                dve.wait_ge(gu_ready, t + 1)
                if not isinstance(t, int) or t >= 3:
                    dve.wait_ge(lo_ready, t - 2)
                nc.vector.scalar_tensor_tensor(out=h32[:, k3, :], in0=gel[:, kp, :], scalar=factor[:, bass.ds(t, 1)], in1=u_ps[kp][:, :],
                                               op0=ALU.mult, op1=ALU.mult).then_inc(h_ready, 1)
                dve.wait_ge(h_ready, t + 1)
                if not isinstance(t, int) or t >= 4:
                    dve.wait_ge(down_done, t - 3)
                nc.vector.tensor_copy(h_hi[:, k4, :], h32[:, k3, :]).then_inc(hi_ready, 1)

            def add_group(j, wait):
                dve.wait_ge(down_done, wait)
                nc.vector.scalar_tensor_tensor(out=acc[:, bass.ds(j * GN, GN)], in0=sh_out[:, :],
                                               scalar=sh_inv[:, bass.ds(j, 1)], in1=acc[:, bass.ds(j * GN, GN)],
                                               op0=ALU.mult, op1=ALU.add).then_inc(added, 1)

            def add_row(b, k, wait):
                dve.wait_ge(down_done, wait)
                if isinstance(b, int) and b == 0:
                    dve.wait_ge(added, G)
                nc.vector.scalar_tensor_tensor(out=acc[:, bass.ds(b * S, S)], in0=row_out[k][:, 0:S],
                                               scalar=sk_inv[:, bass.ds(b, 1)], in1=acc[:, bass.ds(b * S, S)],
                                               op0=ALU.mult, op1=ALU.add).then_inc(added, 1)

            dve.wait_ge(norms, 1)
            nc.vector.tensor_reduce(n_part[:, 0:XC], norm_w[:, NRM_SH:NRM_SK].rearrange("p (q c) -> p q c", q=3), AX.X, ALU.max)
            nc.vector.tensor_reduce(n_part[:, XC:XC + 1], norm_w[:, NRM_X0:NRM_SH], AX.X, ALU.max).then_inc(n_max, 1)
            dve.wait_ge(norms, 2)
            nc.vector.tensor_reduce(n_part[:, XC + 1:KC], norm_x.rearrange("p (j r) -> p j r", r=GR), AX.X,
                                    ALU.max).then_inc(n_max, 1)
            scales(0, 0, XC + 1)
            x_low(0)
            for q in range(3):
                dve.wait_ge(sh_hi_ok, q + 1)
                nc.vector.scalar_tensor_tensor(out=wsh_lo[:, q * I:(q + 1) * I], in0=wsh32[:, q * I:(q + 1) * I],
                                               scalar=sc[:, q:q + 1], in1=wsh_hi[:, q * I:(q + 1) * I],
                                               op0=ALU.mult, op1=ALU.subtract).then_inc(sh_lo_ok, 1)
            shared_tables(0, 0, 1)
            scales(1, XC + 1, KC)
            shared_tables(1, 1, G)
            dve.wait_ge(tab_sh, 2)
            dve.wait_ge(r_routed, 1)
            nc.vector.tensor_copy(wexp[:, :, :], routed[:, :, 0:TOP_K]).then_inc(r_table, 1)
            nc.vector.tensor_scalar(eoff[:, :].rearrange("p (b k) -> p b k", b=B), routed[0:1, :, TOP_K:], float(W), None,
                                    ALU.mult).then_inc(r_table, 1)
            for t in range(SH_STEPS):
                j, c = t // C, t % C
                hidden(t, t % 2, t % 3, t % 4)
                if j == 0:
                    x_low(1 + c)
                elif c == C - 1 and j + C < G:
                    x_low(j + C)
                if c == 1 and j > 0:
                    add_group(j - 1, C * j)
                if t == C * SQ_GROUPS:
                    dve.wait_ge(norms, 2 + SQ_GROUPS)
                    nc.vector.tensor_reduce(n_part[:, KC:NS], norm_w[:, NRM_SK:NRM].rearrange("p (e q c) -> p q e c", e=E, q=3),
                                            AX.XY, ALU.max).then_inc(n_max, 1)
                    scales(2, KC, NS)
                if j >= SQ_GROUPS and c < 3:
                    n = 3 * (j - SQ_GROUPS) + c
                    o = (j - SQ_GROUPS) * (EG * W)
                    hi = wsk_hi[:, o:o + EG * W].rearrange("p (e w) -> p e w", e=EG)[:, :, c * I:(c + 1) * I]
                    lo = wsk_lo[:, o:o + EG * W].rearrange("p (e w) -> p e w", e=EG)[:, :, c * I:(c + 1) * I]
                    w = wsk32[:, o:o + EG * W].rearrange("p (e w) -> p e w", e=EG)[:, :, c * I:(c + 1) * I]
                    dve.wait_ge(sk_hi_ok, n + 1)
                    nc.vector.scalar_tensor_tensor(out=lo, in0=w, scalar=sc[:, KC + c:KC + c + 1], in1=hi,
                                                   op0=ALU.mult, op1=ALU.subtract).then_inc(sk_lo_ok, 1)
                if t == SH_STEPS - 3:
                    ix, sx = inv[:, XC:KC], sc[:, XC:KC]
                    nc.vector.tensor_scalar(tmp_k[:, 0, :], ix, inv[:, KC + 1:KC + 2], 1.0 / HIDDEN_SHIFT,
                                            ALU.mult, ALU.mult).then_inc(t_step, 1)
                    nc.vector.tensor_scalar(tmp_k[:, 1, :], sx, HIDDEN_SHIFT, sc[:, KC:KC + 1], ALU.mult, ALU.mult).then_inc(t_step, 1)
                    per_g = GR * TOP_K
                    sk_gsc = gate_sc[:, SH_STEPS:].rearrange("p (j m) -> p j m", m=per_g)
                    nc.vector.tensor_scalar(sk_gsc, ix.unsqueeze(2).broadcast_to([P, G, per_g]), inv[:, KC:KC + 1], None,
                                            ALU.mult).then_inc(t_step, 1)
                    dve.wait_ge(t_step, 11)
                    nc.vector.tensor_tensor(factor[:, SH_STEPS:].rearrange("p (j m) -> p j m", m=per_g),
                                            tmp_k[:, 1, :].unsqueeze(2).broadcast_to([P, G, per_g]),
                                            wexp[:, :, :].rearrange("p (j r) k -> p j (r k)", r=GR), ALU.mult)
                    nc.vector.scalar_tensor_tensor(out=sk_inv[:, :].rearrange("p (j r) -> p j r", r=GR),
                                                   in0=tmp_k[:, 0, :].unsqueeze(2).broadcast_to([P, G, GR]),
                                                   scalar=inv[:, KC + 2:KC + 3], in1=sk_gsc[:, :, 0:GR],
                                                   op0=ALU.mult, op1=ALU.mult).then_inc(tab_sk, 1)
                    dve.wait_ge(tab_sk, 1)
            for b in range(B):
                for k in range(TOP_K):
                    t = b * TOP_K + k + SH_STEPS
                    hidden(t, t % 2, t % 3, t % 4)
                    if k == 1:
                        if b == 0:
                            add_group(G - 1, SH_STEPS)
                        else:
                            add_row(b - 1, (b - 1) % 2, SH_STEPS + TOP_K * b)
            add_row(B - 1, (B - 1) % 2, SH_STEPS + TOP_K * B)

        @block.tensor
        def _(pe):
            def product(out, w_hi, w_lo, v_hi, v_lo, start, stop):
                nc.tensor.matmul(out, w_hi, v_hi, start=start, stop=False)
                nc.tensor.matmul(out, w_hi, v_lo, start=False, stop=False)
                return nc.tensor.matmul(out, w_lo, v_hi, start=False, stop=stop)

            def norm_columns(out, sq):
                for c in range(out.shape[1]):
                    last = nc.tensor.matmul(out[:, c:c + 1], sq[:, c * P:(c + 1) * P], ones_col[:, :], start=True, stop=True)
                return last

            def norms_skills(n):
                pe.wait_ge(sq_pool, n + 1)
                m = EG * 3 * C
                norm_columns(norm_w[:, NRM_SK + n * m:NRM_SK + (n + 1) * m], sq_sk[:, (n % 2) * EG * W:]).then_inc(norms, 1)

            def gate_up_shared(t, j, c, kp):
                if not isinstance(t, int) or t >= 2:
                    pe.wait_ge(h_ready, t - 1)
                xh, xl = x_hi[:, bass.ds(j * GN, GN)], x_lo[:, bass.ds(j * GN, GN)]
                for out, o in ((g_ps[kp], GATE), (u_ps[kp], UP)):
                    a = o + c * P
                    last = product(out[:, :], wsh_hi[:, a:a + P], wsh_lo[:, a:a + P], xh, xl, True, True)
                last.then_inc(gu_ready, 1)

            def down_shared(t, c, k4):
                pe.wait_ge(hi_ready, t + 1)
                pe.wait_ge(lo_ready, t + 1)
                a = DOWN + c * P
                product(sh_out[:, :], wsh_hi[:, a:a + P], wsh_lo[:, a:a + P], h_hi[:, k4, :], h_lo[:, k4, :],
                        c == 0, c == C - 1).then_inc(down_done, 1)

            def gate_up_skill(b, k):
                e = pe.value_load(eoff[0:1, bass.ds(b * TOP_K + k, 1)], min_val=0, max_val=(E - 1) * W)
                pe.wait_ge(h_ready, b * TOP_K + (SH_STEPS + k - 1))
                xh, xl = x_hi[:, bass.ds(b * S, S)], x_lo[:, bass.ds(b * S, S)]
                for out, o in ((g_ps[k], GATE), (u_ps[k], UP)):
                    for c in range(C):
                        a = e + (o + c * P)
                        last = product(out[:, c * S:(c + 1) * S], wsk_hi[:, bass.ds(a, P)], wsk_lo[:, bass.ds(a, P)],
                                       xh, xl, True, True)
                last.then_inc(gu_ready, 1)

            def down_skill(b, k, par, free=None):
                t = b * TOP_K + (SH_STEPS + k)
                k4 = (TOP_K * par + k) % 4
                e = pe.value_load(eoff[0:1, bass.ds(b * TOP_K + k, 1)], min_val=0, max_val=(E - 1) * W)
                if free is not None:
                    pe.wait_ge(added, free)
                pe.wait_ge(hi_ready, t + 1)
                pe.wait_ge(lo_ready, t + 1)
                for c in range(C):
                    a = e + (DOWN + c * P)
                    last = product(row_out[par][:, 0:S], wsk_hi[:, bass.ds(a, P)], wsk_lo[:, bass.ds(a, P)],
                                   h_hi[:, k4, c * S:(c + 1) * S], h_lo[:, k4, c * S:(c + 1) * S],
                                   k == 0 and c == 0, k == TOP_K - 1 and c == C - 1)
                last.then_inc(down_done, 1)

            pe.wait_ge(consts, 3)
            pe.wait_ge(sq_act, 1)
            norm_columns(norm_w[:, NRM_X0:NRM_SH], sq_x[:, 0:GN])
            pe.wait_ge(sq_act, 2)
            norm_columns(norm_w[:, NRM_SH:NRM_SK], sq_sh[:, :]).then_inc(norms, 1)
            pe.wait_ge(sq_act, 3)
            norm_columns(norm_x, sq_x[:, GN:]).then_inc(norms, 1)
            pe.wait_ge(r_spread, 2 * TOP_K)
            nc.tensor.matmul(row_out[1][:, 0:2 * TOP_K * B], ones32[:, :], spread[:, :, :].rearrange("p b q -> p (b q)"),
                             start=True, stop=True).then_inc(r_routed, 1)
            pe.wait_ge(x_hi_ok, 1)
            pe.wait_ge(x_lo_ok, 1)
            pe.wait_ge(sh_hi_ok, 3)
            pe.wait_ge(sh_lo_ok, 3)
            for c in range(C):
                gate_up_shared(c, 0, c, c % 2)
                if c >= 2:
                    down_shared(c - 2, c - 2, c - 2)
            pe.wait_ge(n_max, 2)
            norms_skills(0)

            def group(j):
                pe.wait_ge(x_hi_ok, j + 1)
                pe.wait_ge(x_lo_ok, j + 1)
                for c in range(C):
                    t = j * C + c
                    gate_up_shared(t, j, c, c % 2)
                    if c == 2:
                        pe.wait_ge(added, j)
                    down_shared(t - 2, (c - 2) % C, (c - 2) % 4)

            for j in range(1, SQ_GROUPS):
                group(j)
                norms_skills(j)
            with pe.Fori(SQ_GROUPS, G) as j:
                group(j)
            pe.wait_ge(r_table, 2)
            pe.wait_ge(sk_hi_ok, 12)
            pe.wait_ge(sk_lo_ok, 12)
            for k in range(TOP_K):
                gate_up_skill(0, k)
                down_shared(SH_STEPS - 2 + k, C - 2 + k, C - 2 + k)
            for k in range(TOP_K):
                gate_up_skill(1, k)
                down_skill(0, k, 0)
            with pe.Fori(0, B // 2 - 1) as i:
                b = i * 2 + 2
                for par in range(2):
                    for k in range(TOP_K):
                        gate_up_skill(b + par, k)
                        down_skill(b + par - 1, k, 1 - par, b + (par + G - 2) if k == 0 else None)
            for k in range(TOP_K):
                down_skill(B - 1, k, 1, G + B - 2)


def kernel(x, cond_8, L0_cond_skill_gate, L0_cond_skill_up, L0_cond_skill_down, L0_cond_shared_gate,
           L0_cond_shared_up, L0_cond_shared_down):
    import numpy as np
    import concourse.bacc as bacc
    from concourse.bass_utils import run_bass_kernel_spmd

    x, cond = np.asarray(x), np.ascontiguousarray(cond_8)
    sg, su, sd = np.asarray(L0_cond_skill_gate), np.asarray(L0_cond_skill_up), np.asarray(L0_cond_skill_down)
    hg, hu, hd = np.asarray(L0_cond_shared_gate), np.asarray(L0_cond_shared_up), np.asarray(L0_cond_shared_down)
    B, S, H = x.shape
    E, _, I = sg.shape
    C = I // 128
    xT = np.ascontiguousarray(x.transpose(2, 0, 1).reshape(H, B * S))
    skills = np.ascontiguousarray(np.concatenate(
        [sg.transpose(1, 0, 2), su.transpose(1, 0, 2),
         sd.reshape(E, C, 128, H).transpose(2, 0, 1, 3).reshape(128, E, C * H)], axis=2).reshape(128, -1))
    shared = np.ascontiguousarray(np.concatenate([hg, hu, hd.reshape(C, 128, H).transpose(1, 0, 2).reshape(128, C * H)], axis=1))
    arrays = {"xT": xT, "cond": cond, "skills": skills, "shared": shared}

    nc = bacc.Bacc("TRN2", target_bir_lowering=False, num_devices=1)
    aps = {n: nc.dram_tensor(n, a.shape, mybir.dt.from_np(a.dtype), kind="ExternalInput").ap() for n, a in arrays.items()}
    outT = nc.dram_tensor("outT", xT.shape, F32, kind="ExternalOutput").ap()
    build(nc, aps["xT"], aps["cond"], aps["skills"], aps["shared"], outT)
    got = run_bass_kernel_spmd(nc, [arrays], core_ids=[0]).results[0]["outT"]
    return np.ascontiguousarray(got.reshape(H, B, S).transpose(1, 2, 0))
```

```python
from contextlib import ExitStack

import concourse.bass as bass
from concourse import mybir

ALU = mybir.AluOpType
ACT = mybir.ActivationFunctionType
AX = mybir.AxisListType
F32 = mybir.dt.float32
F16 = mybir.dt.float16
BF16 = mybir.dt.bfloat16
I32 = mybir.dt.int32
U32 = mybir.dt.uint32
RMAX = bass.bass_isa.ReduceOp.max

P = 128
TOP_K = 2
NUM_MOE_LAYERS = 12

EXP_SHIFT = 24
SCALE_FIELD = 204
INV_FIELD = 254 - SCALE_FIELD
ONE_EXP = float(2 ** 23)
HIDDEN_SHIFT = float(2.0 ** -45)


def build(nc, xT, xS, cond, skills, shared, outS):
    B, E = cond.shape
    H = xT.shape[0]
    S = xT.shape[1] // B
    W = shared.shape[1]
    I = W // 3
    C = I // P
    GR = 512 // S
    G = B // GR
    GN = GR * S
    assert H == P and S == P and I == GN and C == 4 and G == 8 and E == 8
    SPLIT_FROM = 4
    EG = E // (G - SPLIT_FROM)
    W6 = 6
    GATE, UP, DOWN = 0, 2, 4

    ctx = ExitStack()
    with ctx:
        def sb(name, shape, dt):
            return ctx.enter_context(nc.sbuf_tensor(name, shape, dt))

        def ps(name, shape, dt=F32):
            return ctx.enter_context(nc.psum_tensor(name, shape, dt))

        def sem(name):
            return ctx.enter_context(nc.semaphore(name))

        xT32 = sb("xT32", [P, B * S], F32)
        acc = sb("acc", [P, B * H], F32)
        x_hi = sb("x_hi", [P, B * S], F16)
        x_lo = sb("x_lo", [P, B * S], F16)
        wsh32 = sb("wsh32", [P, W], F32)
        wsh = sb("wsh", [P, W6, I], F16)
        wsk32 = sb("wsk32", [P, E * W], F32)
        wsk = sb("wsk", [P, E * W6, I], F16)
        sq_x = sb("sq_x", [P, B * S], BF16)
        sq_w = sb("sq_w", [P, EG * W], BF16)
        ones_col = sb("ones_col", [P, 1], BF16)
        gel = sb("gel", [P, 2, GN], F32)
        h32 = sb("h32", [P, 5, GN], F32)
        h_hi = sb("h_hi", [P, 4, GN], F16)
        h_lo = sb("h_lo", [P, 4, GN], F16)
        NS = 3 + G + 3
        XC, KC = 3, 3 + G
        n_part = sb("n_part", [P, NS], F32)
        n_all = sb("n_all", [P, NS], F32)
        e_half = sb("e_half", [P, NS], U32)
        s_bits = sb("s_bits", [P, NS], I32)
        i_bits = sb("i_bits", [P, NS], I32)
        sc = s_bits[:, :].bitcast(F32)
        inv = i_bits[:, :].bitcast(F32)
        prod = sb("prod", [P, 4], F32)
        T = G * C + B * TOP_K
        gate_sc = sb("gate_sc", [P, T], F32)
        factor = sb("factor", [P, T], F32)
        sh_inv = sb("sh_inv", [P, G], F32)
        sk_inv = sb("sk_inv", [P, B], F32)
        tmp_g = sb("tmp_g", [P, 2, G], F32)
        tmp_k = sb("tmp_k", [P, 2, G], F32)
        logits = sb("logits", [B, E], F32)
        neg_max = sb("neg_max", [B, 1], F32)
        expv = sb("expv", [B, E], F32)
        expsum = sb("expsum", [B, 1], F32)
        rsum = sb("rsum", [B, 1], F32)
        probs = sb("probs", [B, E], F32)
        top_v = sb("top_v", [B, 8], F32)
        top_i = sb("top_i", [B, 8], U32)
        pair = sb("pair", [B, 1], F32)
        rpair = sb("rpair", [B, 1], F32)
        w_raw = sb("w_raw", [B, TOP_K], F32)
        w_live = sb("w_live", [B, TOP_K], F32)
        route = sb("route", [B, 2 * TOP_K], F32)
        ident = sb("ident", [P, P], F32)
        ones32 = sb("ones32", [B, P], F32)
        spread = sb("spread", [B, B, 2 * TOP_K], F32)
        wexp = sb("wexp", [P, B, TOP_K], F32)
        eoff = sb("eoff", [1, B * TOP_K], I32)

        g_ps = [ps(f"g_ps{k}", [P, GN]) for k in range(2)]
        u_ps = [ps(f"u_ps{k}", [P, GN]) for k in range(2)]
        out_ps = [ps(f"out_ps{k}", [P, GN]) for k in range(2)]
        hT_ps = [ps(f"hT_ps{k}", [P, GN]) for k in range(2)]
        NRM_X0, NRM_SH, NRM_SK = 0, GR, GR + 3 * C
        NRM = NRM_SK + E * 3 * C
        norm_w = hT_ps[0]
        norm_x = out_ps[0][:, 0:B - GR]
        route_bc = out_ps[1][:, 0:2 * TOP_K * B]
        routed = route_bc.rearrange("p (b q) -> p b q", b=B)

        cond_in = sem("cond_in")
        x0_in = sem("x0_in")
        xr_in = sem("xr_in")
        sh_in = sem("sh_in")
        sk_in = [sem(f"sk_in{n}") for n in range(E // EG)]
        zeroed = sem("zeroed")
        consts = sem("consts")
        r_negmax = sem("r_negmax")
        r_exp = sem("r_exp")
        r_step = sem("r_step")
        r_spread = sem("r_spread")
        r_routed = sem("r_routed")
        r_table = sem("r_table")
        sq_act = sem("sq_act")
        norms = sem("norms")
        n_max = sem("n_max")
        n_red = sem("n_red")
        s_step = sem("s_step")
        scaled = sem("scaled")
        tab_sh = sem("tab_sh")
        tab_sk = sem("tab_sk")
        t_step = sem("t_step")
        x_hi_ok = sem("x_hi_ok")
        x_lo_ok = sem("x_lo_ok")
        sh_hi_ok = sem("sh_hi_ok")
        sh_lo_ok = sem("sh_lo_ok")
        sk_hi_ok = sem("sk_hi_ok")
        sk_lo_ok = sem("sk_lo_ok")
        gu_ready = sem("gu_ready")
        gelu_ready = sem("gelu_ready")
        h_ready = sem("h_ready")
        hi_ready = sem("hi_ready")
        lo_ready = sem("lo_ready")
        hT_ready = sem("hT_ready")
        skill_hi = sem("skill_hi")
        skill_lo = sem("skill_lo")
        group_done = sem("group_done")
        row_done = sem("row_done")
        xS_in = sem("xS_in")
        added = sem("added")
        half_added = sem("half_added")
        stored = sem("stored")

        LAG = 3
        NORMS_AT = C + E + 1
        SH_STEPS = G * C

        block = ctx.enter_context(nc.Block())

        @block.sync
        def _(sp):
            def load_skills(n):
                sp.dma_start(wsk32[:, n * EG * W:(n + 1) * EG * W], skills[:, n * EG * W:(n + 1) * EG * W]).then_inc(sk_in[n], 16)

            sp.dma_start(logits[:, :], cond).then_inc(cond_in, 16)
            sp.dma_start(xT32[:, 0:GN], xT[:, 0:GN]).then_inc(x0_in, 16)
            sp.dma_start(wsh32[:, :], shared).then_inc(sh_in, 16)
            sp.dma_start(xT32[:, GN:], xT[:, GN:]).then_inc(xr_in, 16)
            load_skills(0)
            sp.dma_start(acc[:, :], xS).then_inc(xS_in, 16)
            for n in range(1, E // EG):
                load_skills(n)
            with sp.Fori(0, G) as j:
                sp.wait_ge(added, GR * j + (G + GR))
                sp.dma_start(outS[:, bass.ds(j * GN, GN)], acc[:, bass.ds(j * GN, GN)]).then_inc(stored, 16)
            sp.wait_ge(stored, 16 * G)

        @block.gpsimd
        def _(pool):
            nc.gpsimd.memset(ones_col[:, :], 1.0).then_inc(consts, 1)
            nc.gpsimd.memset(ones32[:, :], 1.0).then_inc(consts, 1)
            nc.gpsimd.memset(ident[:, :], 0.0).then_inc(zeroed, 1)
            pool.wait_ge(zeroed, 1)
            nc.gpsimd.affine_select(out=ident[:, :], in_=ident[:, :], compare_op=ALU.not_equal, fill=1.0, base=0,
                                    pattern=[[-1, P]], channel_multiplier=1).then_inc(consts, 1)

            def reduce_norms(batch, a, b):
                pool.wait_ge(n_max, batch + 1)
                nc.gpsimd.partition_all_reduce(n_all[:, a:b], n_part[:, a:b], P, RMAX).then_inc(n_red, 1)

            def low_part(t, k3, k4):
                pool.wait_ge(hi_ready, t + 1)
                nc.gpsimd.tensor_tensor(h_lo[:, k4, :], h32[:, k3, :], h_hi[:, k4, :], ALU.subtract).then_inc(lo_ready, 1)

            reduce_norms(0, 0, XC + 1)
            reduce_norms(1, XC + 1, KC)
            for t in range(SH_STEPS):
                low_part(t, t % 3, t % 4)
                if t == NORMS_AT:
                    reduce_norms(2, KC, NS)

        @block.scalar
        def _(act):
            act.wait_ge(r_negmax, 1)
            act.wait_ge(cond_in, 16)
            nc.scalar.activation(expv[:, :], logits[:, :], ACT.Exp, bias=neg_max[:, 0:1],
                                 accum_out=expsum[:, :]).then_inc(r_exp, 1)
            act.wait_ge(x0_in, 16)
            nc.scalar.activation(sq_x[:, 0:GN], xT32[:, 0:GN], ACT.Square).then_inc(sq_act, 1)
            act.wait_ge(sh_in, 16)
            nc.scalar.activation(sq_w[:, 0:W], wsh32[:, :], ACT.Square).then_inc(sq_act, 1)
            act.wait_ge(xr_in, 16)
            nc.scalar.activation(sq_x[:, GN:], xT32[:, GN:], ACT.Square).then_inc(sq_act, 1)

            def x_high(j):
                nc.scalar.activation(x_hi[:, bass.ds(j * GN, GN)], xT32[:, bass.ds(j * GN, GN)], ACT.Copy,
                                     scale=sc[:, bass.ds(XC + j, 1)]).then_inc(x_hi_ok, 1)

            def gelu(t, k):
                act.wait_ge(gu_ready, t + 1)
                nc.scalar.activation(gel[:, k, :], g_ps[k][:, :], ACT.Gelu_apprx_tanh,
                                     scale=gate_sc[:, bass.ds(t, 1)]).then_inc(gelu_ready, 1)

            def square_expert(e):
                act.wait_ge(sk_in[e // EG], 16)
                act.wait_ge(norms, 1 + e)
                o = (e % 2) * W
                nc.scalar.activation(sq_w[:, o:o + W], wsk32[:, e * W:(e + 1) * W], ACT.Square).then_inc(sq_act, 1)

            act.wait_ge(scaled, 1)
            x_high(0)
            for q in range(3):
                nc.scalar.activation(wsh[:, 2 * q, :], wsh32[:, q * I:(q + 1) * I], ACT.Copy,
                                     scale=sc[:, q:q + 1]).then_inc(sh_hi_ok, 1)
            act.wait_ge(tab_sh, 2)
            for c in range(C):
                gelu(c, c % 2)
                x_high(1 + c)
            for t in range(C, SPLIT_FROM * C - 1):
                gelu(t, t % 2)
                if t < C + E:
                    square_expert(t - C)
                else:
                    x_high(t - E + 1)
            for t in range(SPLIT_FROM * C - 1, SPLIT_FROM * C):
                gelu(t, t % 2)
            act.wait_ge(scaled, 3)
            with act.Fori(0, G - SPLIT_FROM) as n:
                w = wsk32[:, :].rearrange("p (e w) -> p e w", e=E)[:, bass.ds(n * EG, EG), :]
                split = wsk[:, :, :].rearrange("p (e m) i -> p e m i", e=E)[:, bass.ds(n * EG, EG), :, :]
                for c in range(C):
                    gelu(n * C + (SPLIT_FROM * C + c), c % 2)
                    if c < 3:
                        nc.scalar.activation(split[:, :, 2 * c, :], w[:, :, c * I:(c + 1) * I], ACT.Copy,
                                             scale=sc[:, KC + c:KC + c + 1]).then_inc(sk_hi_ok, 1)

            def skill_high(u, k, k4):
                act.wait_ge(hT_ready, u + 1)
                nc.scalar.copy(h_hi[:, k4, :], hT_ps[k][:, :]).then_inc(skill_hi, 1)

            act.wait_ge(tab_sk, 1)
            gelu(SH_STEPS, 0)
            gelu(SH_STEPS + 1, 1)
            skill_high(0, 0, 0)
            gelu(SH_STEPS + 2, 0)
            skill_high(1, 1, 1)
            gelu(SH_STEPS + 3, 1)
            with act.Fori(0, B // 2 - 1) as i:
                for v in range(4):
                    skill_high(4 * i + (2 + v), v % 2, (2 + v) % 4)
                    gelu(4 * i + (SH_STEPS + 4 + v), v % 2)
            for v in range(2):
                skill_high(B * TOP_K - 2 + v, v, 2 + v)

        @block.vector
        def _(dve):
            dve.wait_ge(cond_in, 16)
            nc.vector.tensor_reduce(neg_max[:, :], logits[:, :], AX.X, ALU.max, negate=True).then_inc(r_negmax, 1)
            dve.wait_ge(r_exp, 1)
            nc.vector.reciprocal(rsum[:, :], expsum[:, :]).then_inc(r_step, 1)
            dve.wait_ge(r_step, 1)
            nc.vector.tensor_scalar(probs[:, :], expv[:, :], rsum[:, 0:1], None, ALU.mult).then_inc(r_step, 1)
            dve.wait_ge(r_step, 2)
            nc.vector.max(top_v[:, :], probs[:, :]).then_inc(r_step, 1)
            dve.wait_ge(r_step, 3)
            nc.vector.max_index(top_i[:, :], top_v[:, :], probs[:, :]).then_inc(r_step, 1)
            nc.vector.tensor_tensor(pair[:, :], top_v[:, 0:1], top_v[:, 1:2], ALU.add).then_inc(r_step, 1)
            dve.wait_ge(r_step, 5)
            nc.vector.tensor_copy(route[:, TOP_K:], top_i[:, 0:TOP_K]).then_inc(r_step, 1)
            nc.vector.reciprocal(rpair[:, :], pair[:, :]).then_inc(r_step, 1)
            dve.wait_ge(r_step, 7)
            nc.vector.tensor_scalar(w_raw[:, :], top_v[:, 0:TOP_K], rpair[:, 0:1], None, ALU.mult).then_inc(r_step, 1)
            dve.wait_ge(r_step, 8)
            nc.vector.tensor_scalar(w_live[:, :], w_raw[:, :], 1.0 / NUM_MOE_LAYERS, None, ALU.mult).then_inc(r_step, 1)
            dve.wait_ge(r_step, 9)
            nc.vector.scalar_tensor_tensor(out=route[:, 0:TOP_K], in0=w_raw[:, :], scalar=1.0 - 1.0 / NUM_MOE_LAYERS,
                                           in1=w_live[:, :], op0=ALU.mult, op1=ALU.add).then_inc(r_step, 1)
            dve.wait_ge(r_step, 10)
            dve.wait_ge(consts, 3)
            for q in range(2 * TOP_K):
                nc.vector.tensor_scalar(spread[:, :, q], ident[0:B, 0:B], route[:, q:q + 1], None, ALU.mult).then_inc(r_spread, 1)

            def scales(batch, a, b):
                dve.wait_ge(n_red, batch + 1)
                nc.vector.tensor_scalar(e_half[:, a:b], n_all[:, a:b].bitcast(U32), EXP_SHIFT, None,
                                        ALU.logical_shift_right).then_inc(s_step, 1)
                dve.wait_ge(s_step, batch + 1)
                nc.vector.tensor_scalar(i_bits[:, a:b], e_half[:, a:b], ONE_EXP, INV_FIELD * ONE_EXP,
                                        ALU.mult, ALU.add)
                nc.vector.tensor_scalar(s_bits[:, a:b], e_half[:, a:b], -ONE_EXP, SCALE_FIELD * ONE_EXP,
                                        ALU.mult, ALU.add).then_inc(scaled, 1)
                dve.wait_ge(scaled, batch + 1)

            def x_low(j):
                dve.wait_ge(x_hi_ok, j + 1)
                nc.vector.scalar_tensor_tensor(out=x_lo[:, bass.ds(j * GN, GN)], in0=xT32[:, bass.ds(j * GN, GN)],
                                               scalar=sc[:, bass.ds(XC + j, 1)], in1=x_hi[:, bass.ds(j * GN, GN)],
                                               op0=ALU.mult, op1=ALU.subtract).then_inc(x_lo_ok, 1)

            def shared_tables(n, a, b):
                ix, sx = inv[:, XC + a:XC + b], sc[:, XC + a:XC + b]
                n_g = b - a
                nc.vector.tensor_scalar(gate_sc[:, a * C:b * C].rearrange("p (j c) -> p j c", c=C),
                                        ix.unsqueeze(2).broadcast_to([P, n_g, C]), inv[:, 0:1], None, ALU.mult).then_inc(t_step, 1)
                nc.vector.tensor_scalar(factor[:, a * C:b * C].rearrange("p (j c) -> p j c", c=C),
                                        sx.unsqueeze(2).broadcast_to([P, n_g, C]), HIDDEN_SHIFT, sc[:, 0:1],
                                        ALU.mult, ALU.mult).then_inc(t_step, 1)
                nc.vector.tensor_scalar(tmp_g[:, 0, a:b], ix, inv[:, 1:2], 1.0 / HIDDEN_SHIFT,
                                        ALU.mult, ALU.mult).then_inc(t_step, 1)
                dve.wait_ge(t_step, 4 * n + 3)
                nc.vector.tensor_scalar(tmp_g[:, 1, a:b], tmp_g[:, 0, a:b], inv[:, 2:3], None, ALU.mult).then_inc(t_step, 1)
                dve.wait_ge(t_step, 4 * n + 4)
                nc.vector.tensor_tensor(sh_inv[:, a:b], tmp_g[:, 1, a:b], gate_sc[:, a * C:b * C:C], ALU.mult).then_inc(tab_sh, 1)

            def hidden(t, kp, k3):
                dve.wait_ge(gelu_ready, t + 1)
                nc.vector.scalar_tensor_tensor(out=h32[:, k3, :], in0=gel[:, kp, :], scalar=factor[:, bass.ds(t, 1)],
                                               in1=u_ps[kp][:, :], op0=ALU.mult, op1=ALU.mult).then_inc(h_ready, 1)

            def shared_step(t, kp, k3, k4):
                if not isinstance(t, int) or t >= 3:
                    dve.wait_ge(lo_ready, t - 2)
                hidden(t, kp, k3)
                dve.wait_ge(h_ready, t + 1)
                nc.vector.tensor_copy(h_hi[:, k4, :], h32[:, k3, :]).then_inc(hi_ready, 1)

            def skill_low(u, k, k4):
                dve.wait_ge(skill_hi, u + 1)
                nc.vector.tensor_tensor(h_lo[:, k4, :], hT_ps[k][:, :], h_hi[:, k4, :], ALU.subtract).then_inc(skill_lo, 1)

            def add_group(j, par):
                group = acc[:, bass.ds(j * GN, GN)]
                dve.wait_ge(group_done, j + 1)
                nc.vector.scalar_tensor_tensor(out=group, in0=out_ps[par][:, :], scalar=sh_inv[:, bass.ds(j, 1)], in1=group,
                                               op0=ALU.mult, op1=ALU.add).then_inc(added, 1)

            def add_row(b, k):
                row = acc[:, bass.ds(b * H, H)]
                dve.wait_ge(row_done, b + 1)
                nc.vector.scalar_tensor_tensor(out=row, in0=out_ps[k][:, 0:H], scalar=sk_inv[:, bass.ds(b, 1)], in1=row,
                                               op0=ALU.mult, op1=ALU.add).then_inc(half_added, 1)
                dve.wait_ge(half_added, b + 1)
                nc.vector.scalar_tensor_tensor(out=row, in0=out_ps[k][:, H:2 * H], scalar=sk_inv[:, bass.ds(b, 1)], in1=row,
                                               op0=ALU.mult, op1=ALU.add).then_inc(added, 1)

            dve.wait_ge(norms, 1)
            nc.vector.tensor_reduce(n_part[:, 0:XC], norm_w[:, NRM_SH:NRM_SK].rearrange("p (q c) -> p q c", q=3), AX.X, ALU.max)
            nc.vector.tensor_reduce(n_part[:, XC:XC + 1], norm_w[:, NRM_X0:NRM_SH], AX.X, ALU.max).then_inc(n_max, 1)
            dve.wait_ge(norms, 2)
            nc.vector.tensor_reduce(n_part[:, XC + 1:KC], norm_x.rearrange("p (j r) -> p j r", r=GR), AX.X,
                                    ALU.max).then_inc(n_max, 1)
            scales(0, 0, XC + 1)
            x_low(0)
            for q in range(3):
                dve.wait_ge(sh_hi_ok, q + 1)
                nc.vector.scalar_tensor_tensor(out=wsh[:, 2 * q + 1, :], in0=wsh32[:, q * I:(q + 1) * I],
                                               scalar=sc[:, q:q + 1], in1=wsh[:, 2 * q, :],
                                               op0=ALU.mult, op1=ALU.subtract).then_inc(sh_lo_ok, 1)
            shared_tables(0, 0, 1)
            scales(1, XC + 1, KC)
            shared_tables(1, 1, G)
            dve.wait_ge(tab_sh, 2)
            dve.wait_ge(r_routed, 1)
            nc.vector.tensor_copy(wexp[:, :, :], routed[:, :, 0:TOP_K]).then_inc(r_table, 1)
            nc.vector.tensor_scalar(eoff[:, :].rearrange("p (b k) -> p b k", b=B), routed[0:1, :, TOP_K:], float(W6), None,
                                    ALU.mult).then_inc(r_table, 1)
            for t in range(SH_STEPS):
                j, c = t // C, t % C
                shared_step(t, t % 2, t % 3, t % 4)
                if t < C:
                    x_low(1 + t)
                elif C + E <= t < SPLIT_FROM * C - 1:
                    x_low(t - E + 1)
                if c == 2 and j > 0:
                    if j == 1:
                        dve.wait_ge(xS_in, 16)
                    add_group(j - 1, (j - 1) % 2)
                if t == NORMS_AT:
                    dve.wait_ge(norms, 2 + E)
                    nc.vector.tensor_reduce(n_part[:, KC:NS], norm_w[:, NRM_SK:NRM].rearrange("p (e q c) -> p q e c", e=E, q=3),
                                            AX.XY, ALU.max).then_inc(n_max, 1)
                if t == NORMS_AT + 1:
                    scales(2, KC, NS)
                if j >= SPLIT_FROM and c < 3:
                    n, e = j - SPLIT_FROM, (j - SPLIT_FROM) * EG
                    split = wsk[:, e * W6:(e + EG) * W6, :].rearrange("p (e m) i -> p e m i", e=EG)
                    w = wsk32[:, e * W:(e + EG) * W].rearrange("p (e w) -> p e w", e=EG)[:, :, c * I:(c + 1) * I]
                    dve.wait_ge(sk_hi_ok, 3 * n + c + 1)
                    nc.vector.scalar_tensor_tensor(out=split[:, :, 2 * c + 1, :], in0=w, scalar=sc[:, KC + c:KC + c + 1],
                                                   in1=split[:, :, 2 * c, :], op0=ALU.mult, op1=ALU.subtract).then_inc(sk_lo_ok, 1)
                if t == SH_STEPS - 3:
                    ix, sx = inv[:, XC:KC], sc[:, XC:KC]
                    nc.vector.tensor_scalar(tmp_k[:, 0, :], ix, inv[:, KC + 1:KC + 2], 1.0 / HIDDEN_SHIFT,
                                            ALU.mult, ALU.mult).then_inc(t_step, 1)
                    nc.vector.tensor_scalar(tmp_k[:, 1, :], sx, HIDDEN_SHIFT, sc[:, KC:KC + 1], ALU.mult, ALU.mult).then_inc(t_step, 1)
                    per_g = GR * TOP_K
                    sk_gsc = gate_sc[:, SH_STEPS:].rearrange("p (j m) -> p j m", m=per_g)
                    nc.vector.tensor_scalar(sk_gsc, ix.unsqueeze(2).broadcast_to([P, G, per_g]), inv[:, KC:KC + 1], None,
                                            ALU.mult).then_inc(t_step, 1)
                    dve.wait_ge(t_step, 11)
                    nc.vector.tensor_tensor(factor[:, SH_STEPS:].rearrange("p (j m) -> p j m", m=per_g),
                                            tmp_k[:, 1, :].unsqueeze(2).broadcast_to([P, G, per_g]),
                                            wexp[:, :, :].rearrange("p (j r) k -> p j (r k)", r=GR), ALU.mult)
                    nc.vector.scalar_tensor_tensor(out=sk_inv[:, :].rearrange("p (j r) -> p j r", r=GR),
                                                   in0=tmp_k[:, 0, :].unsqueeze(2).broadcast_to([P, G, GR]),
                                                   scalar=inv[:, KC + 2:KC + 3], in1=sk_gsc[:, :, 0:GR],
                                                   op0=ALU.mult, op1=ALU.mult).then_inc(tab_sk, 1)
                    dve.wait_ge(tab_sk, 1)
            hidden(SH_STEPS, 0, 3)
            hidden(SH_STEPS + 1, 1, 4)
            skill_low(0, 0, 0)
            hidden(SH_STEPS + 2, 0, 3)
            add_group(G - 1, 1)
            skill_low(1, 1, 1)
            hidden(SH_STEPS + 3, 1, 4)
            with dve.Fori(0, B // 2 - 1) as i:
                for v in range(4):
                    skill_low(4 * i + (2 + v), v % 2, (2 + v) % 4)
                    hidden(4 * i + (SH_STEPS + 4 + v), v % 2, 3 + v % 2)
                    if v % 2 == 0:
                        add_row(2 * i + v // 2, v // 2)
            for v in range(2):
                skill_low(B * TOP_K - 2 + v, v, 2 + v)
            for v in range(2):
                add_row(B - 2 + v, v)

        @block.tensor
        def _(pe):
            def norm_columns(out, sq):
                for c in range(out.shape[1]):
                    last = nc.tensor.matmul(out[:, c:c + 1], sq[:, c * P:(c + 1) * P], ones_col[:, :], start=True, stop=True)
                return last

            def norms_expert(e):
                pe.wait_ge(sq_act, 4 + e)
                m, o = 3 * C, (e % 2) * W
                norm_columns(norm_w[:, NRM_SK + e * m:NRM_SK + (e + 1) * m], sq_w[:, o:o + W]).then_inc(norms, 1)

            def gate_up_shared(t, j, c, kp):
                if not isinstance(t, int) or t >= 2:
                    pe.wait_ge(h_ready, t - 1)
                xh, xl = x_hi[:, bass.ds(j * GN, GN)], x_lo[:, bass.ds(j * GN, GN)]
                for out, m in ((g_ps[kp], GATE), (u_ps[kp], UP)):
                    w_hi, w_lo = wsh[:, m, c * P:(c + 1) * P], wsh[:, m + 1, c * P:(c + 1) * P]
                    nc.tensor.matmul(out[:, :], w_hi, xh, start=True, stop=False)
                    nc.tensor.matmul(out[:, :], w_hi, xl, start=False, stop=False)
                    last = nc.tensor.matmul(out[:, :], w_lo, xh, start=False, stop=True)
                last.then_inc(gu_ready, 1)

            def down_shared(t, par, c, k4, free=None):
                if free is not None:
                    pe.wait_ge(added, free)
                pe.wait_ge(lo_ready, t + 1)
                w_hi, w_lo = wsh[:, DOWN, c * P:(c + 1) * P], wsh[:, DOWN + 1, c * P:(c + 1) * P]
                for r in range(GR):
                    out, rows = out_ps[par][:, r * H:(r + 1) * H], slice(r * S, (r + 1) * S)
                    hi, lo = h_hi[:, k4, rows], h_lo[:, k4, rows]
                    nc.tensor.matmul(out, hi, w_hi, start=(c == 0 and r == 0), stop=False, skip_group_check=True)
                    nc.tensor.matmul(out, hi, w_lo, start=False, stop=False, skip_group_check=True)
                    last = nc.tensor.matmul(out, lo, w_hi, start=False, stop=(c == C - 1), skip_group_check=True)
                if c == C - 1:
                    last.then_inc(group_done, 1)

            def experts(first, n):
                _, e = nc.values_load_multi_w_load_instructions(
                    eoff[0:1, bass.ds(first, n)], engines=[pe.engine], min_val=0, max_val=(E - 1) * W6,
                    skip_runtime_bounds_check_because="the indices of the largest of E probabilities are 0 to E - 1")
                return e

            def gate_up_skill(b, k, e):
                xh, xl = x_hi[:, bass.ds(b * S, S)], x_lo[:, bass.ds(b * S, S)]
                for out, m in ((g_ps[k], GATE), (u_ps[k], UP)):
                    w_hi, w_lo = wsk[:, bass.ds(e + m, 1), :], wsk[:, bass.ds(e + (m + 1), 1), :]
                    nc.tensor.matmul(out[:, :], xh, w_hi, start=True, stop=False)
                    nc.tensor.matmul(out[:, :], xl, w_hi, start=False, stop=False)
                    last = nc.tensor.matmul(out[:, :], xh, w_lo, start=False, stop=True)
                last.then_inc(gu_ready, 1)

            def turn_skill(u, k):
                pe.wait_ge(h_ready, u + (SH_STEPS + 1))
                for c in range(C):
                    last = nc.tensor.transpose(hT_ps[k][:, c * S:(c + 1) * S], h32[:, 3 + k, c * P:(c + 1) * P], ident[:, :])
                last.then_inc(hT_ready, 1)

            def down_skill(b, k, par, e):
                k4 = (TOP_K * par + k) % 4
                pe.wait_ge(skill_lo, b * TOP_K + (k + 1))
                for c in range(C):
                    first, final = k == 0 and c == 0, k == TOP_K - 1 and c == C - 1
                    w_pair = wsk[:, bass.ds(e + DOWN, 2), c * P:(c + 1) * P]
                    hi, lo = h_hi[:, k4, c * S:(c + 1) * S], h_lo[:, k4, c * S:(c + 1) * S]
                    nc.tensor.matmul(out_ps[par][:, 0:2 * H], hi, w_pair, start=first, stop=final, skip_group_check=True)
                    last = nc.tensor.matmul(out_ps[par][:, 0:H], lo, w_pair[:, 0, :], start=False, stop=final,
                                            skip_group_check=True)
                if k == TOP_K - 1:
                    last.then_inc(row_done, 1)

            pe.wait_ge(consts, 3)
            pe.wait_ge(sq_act, 1)
            norm_columns(norm_w[:, NRM_X0:NRM_SH], sq_x[:, 0:GN])
            pe.wait_ge(sq_act, 2)
            norm_columns(norm_w[:, NRM_SH:NRM_SK], sq_w[:, 0:W]).then_inc(norms, 1)
            pe.wait_ge(sq_act, 3)
            norm_columns(norm_x, sq_x[:, GN:]).then_inc(norms, 1)
            pe.wait_ge(r_spread, 2 * TOP_K)
            nc.tensor.matmul(route_bc, ones32[:, :], spread[:, :, :].rearrange("p b q -> p (b q)"),
                             start=True, stop=True).then_inc(r_routed, 1)
            pe.wait_ge(x_lo_ok, 1)
            pe.wait_ge(sh_lo_ok, 2)
            for c in range(C):
                gate_up_shared(c, 0, c, c % 2)
                if c == LAG:
                    pe.wait_ge(n_max, 2)
                    pe.wait_ge(r_table, 2)
                    pe.wait_ge(sh_lo_ok, 3)
                    down_shared(0, 0, 0, 0)

            def group(j, par, norms_from=None):
                pe.wait_ge(x_lo_ok, j + 1)
                for c in range(C):
                    t = j * C + c
                    gate_up_shared(t, j, c, c % 2)
                    down_shared(t - LAG, par if c >= LAG else 1 - par, (c - LAG) % C, (c - LAG) % 4,
                                j - 1 if c == LAG and (not isinstance(j, int) or j >= 2) else None)
                    if norms_from is not None and 0 <= t - norms_from < E:
                        norms_expert(t - norms_from)

            for j in range(1, SPLIT_FROM):
                group(j, j % 2, C + 1)
            with pe.Fori(0, (G - SPLIT_FROM) // 2) as n:
                for par in range(2):
                    group(2 * n + (SPLIT_FROM + par), par)
            pe.wait_ge(sk_lo_ok, 3 * (G - SPLIT_FROM))
            pe.wait_ge(h_ready, SH_STEPS)
            e = experts(0, 2 * TOP_K)
            for u in range(LAG):
                gate_up_skill(u // TOP_K, u % TOP_K, e[u])
                down_shared(SH_STEPS - LAG + u, 1, C - LAG + u, C - LAG + u)
                if u >= 1:
                    turn_skill(u - 1, (u - 1) % 2)
            gate_up_skill(LAG // TOP_K, LAG % TOP_K, e[LAG])
            down_skill(0, 0, 0, e[0])
            turn_skill(LAG - 1, (LAG - 1) % 2)
            with pe.Fori(0, B // 2 - 1) as i:
                e = experts(4 * i + 1, LAG + 4)
                for v in range(4):
                    gate_up_skill(2 * i + (2 + v // TOP_K), v % TOP_K, e[LAG + v])
                    down_skill(2 * i + (1 + v) // TOP_K, (1 + v) % TOP_K, (1 + v) // TOP_K % 2, e[v])
                    turn_skill(4 * i + (3 + v), (3 + v) % 2)
            e = experts(TOP_K * B - LAG, LAG)
            down_skill(B - 2, 1, 0, e[0])
            turn_skill(B * TOP_K - 1, 1)
            for k in range(TOP_K):
                down_skill(B - 1, k, 1, e[1 + k])


def kernel(x, cond_8, L0_cond_skill_gate, L0_cond_skill_up, L0_cond_skill_down, L0_cond_shared_gate,
           L0_cond_shared_up, L0_cond_shared_down):
    import numpy as np
    import concourse.bacc as bacc
    from concourse.bass_utils import run_bass_kernel_spmd

    x, cond = np.asarray(x), np.ascontiguousarray(cond_8)
    sg, su, sd = np.asarray(L0_cond_skill_gate), np.asarray(L0_cond_skill_up), np.asarray(L0_cond_skill_down)
    hg, hu, hd = np.asarray(L0_cond_shared_gate), np.asarray(L0_cond_shared_up), np.asarray(L0_cond_shared_down)
    B, S, H = x.shape
    E, _, I = sg.shape
    C = I // 128
    xT = np.ascontiguousarray(x.transpose(2, 0, 1).reshape(H, B * S))
    skills = np.ascontiguousarray(np.concatenate(
        [sg.transpose(1, 0, 2), su.transpose(1, 0, 2),
         sd.reshape(E, C, 128, H).transpose(2, 0, 1, 3).reshape(128, E, C * H)], axis=2).reshape(128, -1))
    shared = np.ascontiguousarray(np.concatenate([hg, hu, hd.reshape(C, 128, H).transpose(1, 0, 2).reshape(128, C * H)], axis=1))
    xS = np.ascontiguousarray(x.transpose(1, 0, 2).reshape(S, B * H))
    arrays = {"xT": xT, "xS": xS, "cond": cond, "skills": skills, "shared": shared}

    nc = bacc.Bacc("TRN2", target_bir_lowering=False, num_devices=1)
    aps = {n: nc.dram_tensor(n, a.shape, mybir.dt.from_np(a.dtype), kind="ExternalInput").ap() for n, a in arrays.items()}
    outS = nc.dram_tensor("outS", xS.shape, F32, kind="ExternalOutput").ap()
    build(nc, aps["xT"], aps["xS"], aps["cond"], aps["skills"], aps["shared"], outS)
    got = run_bass_kernel_spmd(nc, [arrays], core_ids=[0]).results[0]["outS"]
    return np.ascontiguousarray(got.reshape(S, B, H).transpose(1, 0, 2))
```

```python
from contextlib import ExitStack

import concourse.bass as bass
from concourse import mybir

ALU = mybir.AluOpType
ACT = mybir.ActivationFunctionType
AX = mybir.AxisListType
F32 = mybir.dt.float32
F16 = mybir.dt.float16
BF16 = mybir.dt.bfloat16
I32 = mybir.dt.int32
U32 = mybir.dt.uint32
RMAX = bass.bass_isa.ReduceOp.max

P = 128
TOP_K = 2
NUM_MOE_LAYERS = 12

EXP_SHIFT = 24
SCALE_FIELD = 204
INV_FIELD = 254 - SCALE_FIELD
ONE_EXP = float(2 ** 23)
HIDDEN_SHIFT = float(2.0 ** -45)


def build(nc, xT, xS, cond, skills, shared, outS):
    B, E = cond.shape
    H = xT.shape[0]
    S = xT.shape[1] // B
    W = shared.shape[1]
    I = W // 3
    C = I // P
    GR = 512 // S
    G = B // GR
    GN = GR * S
    assert H == P and S == P and I == GN and C == 4 and G == 8 and E == 8
    SPLIT_FROM = 4
    EG = E // (G - SPLIT_FROM)
    W6 = 6
    GATE, UP, DOWN = 0, 2, 4

    ctx = ExitStack()
    with ctx:
        def sb(name, shape, dt):
            return ctx.enter_context(nc.sbuf_tensor(name, shape, dt))

        def ps(name, shape, dt=F32):
            return ctx.enter_context(nc.psum_tensor(name, shape, dt))

        def sem(name):
            return ctx.enter_context(nc.semaphore(name))

        xT32 = sb("xT32", [P, B * S], F32)
        acc = sb("acc", [P, B * H], F32)
        x_hi = sb("x_hi", [P, B * S], F16)
        x_lo = sb("x_lo", [P, B * S], F16)
        wsh32 = sb("wsh32", [P, W], F32)
        wsh = sb("wsh", [P, W6, I], F16)
        wsk32 = sb("wsk32", [P, E * W], F32)
        wsk_gu = [[sb(f"wsk_{m}{c}", [P, E * P], F16) for c in range(C)] for m in ("gate_hi", "gate_lo", "up_hi", "up_lo")]
        wsk_down = [sb(f"wsk_down{c}", [P, 2, E * P], F16) for c in range(C)]
        sq_x = sb("sq_x", [P, B * S], BF16)
        sq_w = sb("sq_w", [P, EG * W], BF16)
        ones_col = sb("ones_col", [P, 1], BF16)
        zeros = sb("zeros", [P, GN], BF16)
        gel = sb("gel", [P, 2, GN], F32)
        h32 = sb("h32", [P, 4, GN], F32)
        h_hi = sb("h_hi", [P, 4, GN], F16)
        h_lo = sb("h_lo", [P, 4, GN], F16)
        NS = 1 + G + 2 + 3
        GC, XC, UC, DC, KC = 0, 1, 1 + G, 2 + G, 3 + G
        XA = 4
        BATCHES = [(0, XC + 1), (UC, KC), (XC + 1, XC + XA), (XC + XA, UC), (KC, NS)]
        FIRST, UP_DOWN, X_NEXT, X_REST, SKILLS = range(5)
        n_part = sb("n_part", [P, NS], F32)
        n_all = sb("n_all", [P, NS], F32)
        e_half = sb("e_half", [P, NS], U32)
        s_bits = sb("s_bits", [P, NS], I32)
        i_bits = sb("i_bits", [P, NS], I32)
        sc = s_bits[:, :].bitcast(F32)
        inv = i_bits[:, :].bitcast(F32)
        prod = sb("prod", [P, 4], F32)
        T = G * C + B * TOP_K
        gate_sc = sb("gate_sc", [P, T], F32)
        factor = sb("factor", [P, T], F32)
        sh_inv = sb("sh_inv", [P, G], F32)
        sk_inv = sb("sk_inv", [P, B], F32)
        tmp_g = sb("tmp_g", [P, 2, G], F32)
        warm = sb("warm", [B, 2], F32)
        tmp_k = sb("tmp_k", [P, 2, G], F32)
        logits = sb("logits", [B, E], F32)
        neg_max = sb("neg_max", [B, 1], F32)
        expv = sb("expv", [B, E], F32)
        expsum = sb("expsum", [B, 1], F32)
        rsum = sb("rsum", [B, 1], F32)
        probs = sb("probs", [B, E], F32)
        top_v = sb("top_v", [B, 8], F32)
        top_i = sb("top_i", [B, 8], U32)
        pair = sb("pair", [B, 1], F32)
        rpair = sb("rpair", [B, 1], F32)
        w_raw = sb("w_raw", [B, TOP_K], F32)
        w_live = sb("w_live", [B, TOP_K], F32)
        route = sb("route", [B, 2 * TOP_K], F32)
        ident = sb("ident", [P, P], F32)
        ones32 = sb("ones32", [B, P], F32)
        spread = sb("spread", [B, B, 2 * TOP_K], F32)
        wexp = sb("wexp", [P, B, TOP_K], F32)
        eoff = sb("eoff", [1, B * TOP_K], I32)

        g_ps = [ps(f"g_ps{k}", [P, GN]) for k in range(2)]
        u_ps = [ps(f"u_ps{k}", [P, GN]) for k in range(2)]
        out_ps = [ps(f"out_ps{k}", [P, GN]) for k in range(2)]
        norm_ps = ps("norm_ps", [P, GN])
        route_ps = ps("route_ps", [P, GN])
        NRM_X0, NRM_XR = C, C + GR
        NRM_SK = NRM_XR + (G - XA) * GR
        NRM = NRM_SK + E * 3 * C
        norm_ud, norm_xn = out_ps[0][:, 0:2 * C], out_ps[1][:, 0:(XA - 1) * GR]
        route_bc = route_ps[:, 0:2 * TOP_K * B]
        routed = route_bc.rearrange("p (b q) -> p b q", b=B)

        cond_in = sem("cond_in")
        x0_in = sem("x0_in")
        xn_in = sem("xn_in")
        xr_in = sem("xr_in")
        shg_in = sem("shg_in")
        shud_in = sem("shud_in")
        sk_in = [sem(f"sk_in{n}") for n in range(E // EG)]
        zeros_ok = sem("zeros_ok")
        zeroed = sem("zeroed")
        consts = sem("consts")
        r_negmax = sem("r_negmax")
        r_exp = sem("r_exp")
        r_step = sem("r_step")
        r_spread = sem("r_spread")
        r_routed = sem("r_routed")
        r_table = sem("r_table")
        sq_act = sem("sq_act")
        norms = sem("norms")
        n_max = sem("n_max")
        n_red = sem("n_red")
        s_step = sem("s_step")
        scaled = sem("scaled")
        tab_sh = sem("tab_sh")
        tab_sk = sem("tab_sk")
        t_step = sem("t_step")
        x_hi_ok = sem("x_hi_ok")
        x_lo_ok = sem("x_lo_ok")
        sh_hi_ok = sem("sh_hi_ok")
        sh_lo_ok = sem("sh_lo_ok")
        sk_hi_ok = sem("sk_hi_ok")
        sk_lo_ok = sem("sk_lo_ok")
        gu_ready = sem("gu_ready")
        gelu_ready = sem("gelu_ready")
        h_ready = sem("h_ready")
        hi_ready = sem("hi_ready")
        hi_act = sem("hi_act")
        lo_ready = sem("lo_ready")
        last_lo = sem("last_lo")
        group_done = sem("group_done")
        row_done = sem("row_done")
        xS_in = sem("xS_in")
        added = sem("added")
        half_added = sem("half_added")
        stored = sem("stored")

        WARM_BEFORE, WARM_SPLIT, WARM_AFTER = 9, 0, 3
        LAG = 3
        SQ_FROM = 7
        NORMS_AT = SQ_FROM + E
        SH_STEPS = G * C
        STEPS = SH_STEPS + B * TOP_K
        SK_GU = 2 * C
        PIECE_STEPS = [17, 19, 20, 21, 23, 24, 25, 27, 28, 29, 31, 32]
        PIECES = {t: (n % 2, n // 2) if n < SK_GU else (2, n - SK_GU) for n, t in enumerate(PIECE_STEPS)}

        def skill_piece(q, c):
            w = wsk32[:, :].rearrange("p (e w) -> p e w", e=E)[:, :, q * I + c * P:q * I + (c + 1) * P]
            hi, lo = (wsk_down[c][:, 0, :], wsk_down[c][:, 1, :]) if q == 2 else (wsk_gu[2 * q][c][:, :], wsk_gu[2 * q + 1][c][:, :])
            return w, hi.rearrange("p (e i) -> p e i", e=E), lo.rearrange("p (e i) -> p e i", e=E)

        def hi_on_act(t):
            return PIECE_STEPS[0] <= t < SH_STEPS + 2 and t % C != C - 1

        ACT_HIGHS = sum(hi_on_act(t) for t in range(STEPS))

        block = ctx.enter_context(nc.Block())

        @block.sync
        def _(sp):
            def load_skills(n):
                sp.dma_start(wsk32[:, n * EG * W:(n + 1) * EG * W], skills[:, n * EG * W:(n + 1) * EG * W]).then_inc(sk_in[n], 16)

            sp.dma_start(logits[:, :], cond).then_inc(cond_in, 16)
            sp.dma_start(xT32[:, 0:GN], xT[:, 0:GN]).then_inc(x0_in, 16)
            sp.dma_start(wsh32[:, 0:I], shared[:, 0:I]).then_inc(shg_in, 16)
            sp.dma_start(wsh32[:, I:W], shared[:, I:W]).then_inc(shud_in, 16)
            sp.dma_start(xT32[:, GN:XA * GN], xT[:, GN:XA * GN]).then_inc(xn_in, 16)
            sp.dma_start(xT32[:, XA * GN:], xT[:, XA * GN:]).then_inc(xr_in, 16)
            load_skills(0)
            sp.dma_start(acc[:, :], xS).then_inc(xS_in, 16)
            for n in range(1, E // EG):
                load_skills(n)
            with sp.Fori(0, G - 1) as j:
                sp.wait_ge(added, GR * j + (G + GR))
                sp.dma_start(outS[:, bass.ds(j * GN, GN)], acc[:, bass.ds(j * GN, GN)]).then_inc(stored, 16)
            for a, b in ((B - GR, B - 1), (B - 1, B)):
                sp.wait_ge(added, G + b)
                sp.dma_start(outS[:, a * H:b * H], acc[:, a * H:b * H]).then_inc(stored, 16)
            sp.wait_ge(stored, 16 * (G + 1))

        @block.gpsimd
        def _(pool):
            nc.gpsimd.memset(zeros[:, :], 0.0).then_inc(zeros_ok, 1)
            nc.gpsimd.memset(ones_col[:, :], 1.0).then_inc(consts, 1)
            nc.gpsimd.memset(ones32[:, :], 1.0).then_inc(consts, 1)
            nc.gpsimd.memset(ident[:, :], 0.0).then_inc(zeroed, 1)
            pool.wait_ge(zeroed, 1)
            nc.gpsimd.affine_select(out=ident[:, :], in_=ident[:, :], compare_op=ALU.not_equal, fill=1.0, base=0,
                                    pattern=[[-1, P]], channel_multiplier=1).then_inc(consts, 1)

            def reduce_norms(batch):
                a, b = BATCHES[batch]
                pool.wait_ge(n_max, batch + 1)
                nc.gpsimd.partition_all_reduce(n_all[:, a:b], n_part[:, a:b], P, RMAX).then_inc(n_red, 1)

            def low_part(k4):
                nc.gpsimd.tensor_tensor(h_lo[:, k4, :], h32[:, k4, :], h_hi[:, k4, :], ALU.subtract).then_inc(lo_ready, 1)

            reduce_norms(FIRST)
            reduce_norms(UP_DOWN)
            reduce_norms(X_NEXT)
            n_act = 0
            for t in range(SH_STEPS + 4):
                if hi_on_act(t):
                    n_act += 1
                    pool.wait_ge(hi_act, n_act)
                else:
                    pool.wait_ge(hi_ready, t + 1 - n_act)
                low_part(t % 4)
                if t == 4:
                    reduce_norms(X_REST)
                if t == NORMS_AT:
                    reduce_norms(SKILLS)
            with pool.Fori(0, B // 2 - 2) as i:
                for v in range(4):
                    pool.wait_ge(hi_ready, 4 * i + (SH_STEPS - ACT_HIGHS + 5 + v))
                    low_part(v)
            for v in range(3):
                pool.wait_ge(hi_ready, STEPS - ACT_HIGHS - 3 + v)
                low_part(v)

        @block.scalar
        def _(act):
            act.wait_ge(consts, 2)
            nc.scalar.activation(warm[:, 0:1], ones32[:, 0:1], ACT.Exp)
            act.wait_ge(r_negmax, 1)
            act.wait_ge(cond_in, 16)
            nc.scalar.activation(expv[:, :], logits[:, :], ACT.Exp, bias=neg_max[:, 0:1],
                                 accum_out=expsum[:, :]).then_inc(r_exp, 1)
            nc.scalar.activation(warm[:, 1:2], ones32[:, 0:1], ACT.Gelu_apprx_tanh)
            act.wait_ge(x0_in, 16)
            nc.scalar.activation(sq_x[:, 0:GN], xT32[:, 0:GN], ACT.Square).then_inc(sq_act, 1)
            act.wait_ge(shg_in, 16)
            nc.scalar.activation(sq_w[:, 0:I], wsh32[:, 0:I], ACT.Square).then_inc(sq_act, 1)
            act.wait_ge(shud_in, 16)
            nc.scalar.activation(sq_w[:, I:W], wsh32[:, I:W], ACT.Square).then_inc(sq_act, 1)
            def x_high(j):
                nc.scalar.activation(x_hi[:, bass.ds(j * GN, GN)], xT32[:, bass.ds(j * GN, GN)], ACT.Copy,
                                     scale=sc[:, bass.ds(XC + j, 1)]).then_inc(x_hi_ok, 1)

            def gelu(t, k):
                act.wait_ge(gu_ready, t + 1)
                nc.scalar.activation(gel[:, k, :], g_ps[k][:, :], ACT.Gelu_apprx_tanh,
                                     scale=gate_sc[:, bass.ds(t, 1)]).then_inc(gelu_ready, 1)

            def square_expert(e):
                act.wait_ge(sk_in[e // EG], 16)
                act.wait_ge(norms, max(3 + e, 4))
                o = (e % 2) * W
                nc.scalar.activation(sq_w[:, o:o + W], wsk32[:, e * W:(e + 1) * W], ACT.Square).then_inc(sq_act, 1)

            def shared_high(q):
                nc.scalar.activation(wsh[:, 2 * q, :], wsh32[:, q * I:(q + 1) * I], ACT.Copy,
                                     scale=sc[:, (GC, UC, DC)[q]:(GC, UC, DC)[q] + 1]).then_inc(sh_hi_ok, 1)

            def high_part(t):
                act.wait_ge(h_ready, t + 1)
                nc.scalar.copy(h_hi[:, t % 4, :], h32[:, t % 4, :]).then_inc(hi_act, 1)

            def split_high(q, c):
                w, hi, _ = skill_piece(q, c)
                nc.scalar.activation(hi, w, ACT.Copy, scale=sc[:, KC + q:KC + q + 1]).then_inc(sk_hi_ok, 1)

            def square_x(a, b):
                nc.scalar.activation(sq_x[:, a * GN:b * GN], xT32[:, a * GN:b * GN], ACT.Square).then_inc(sq_act, 1)

            act.wait_ge(scaled, FIRST + 1)
            shared_high(0)
            act.wait_ge(scaled, UP_DOWN + 1)
            shared_high(1)
            act.wait_ge(xn_in, 16)
            square_x(1, XA)
            act.wait_ge(tab_sh, 1)
            for t in range(SH_STEPS):
                if t == C:
                    act.wait_ge(tab_sh, 2)
                if t == XA * C:
                    act.wait_ge(tab_sh, 3)
                gelu(t, t % 2)
                if t == 0:
                    shared_high(2)
                if t == 1:
                    act.wait_ge(scaled, X_NEXT + 1)
                    x_high(1)
                if t == 2:
                    act.wait_ge(xr_in, 16)
                    square_x(XA, XA + 2)
                if t == 3:
                    square_x(XA + 2, G)
                if t == 4:
                    x_high(2)
                    x_high(3)
                if t == 6:
                    act.wait_ge(scaled, X_REST + 1)
                    x_high(4)
                    x_high(5)
                if t == NORMS_AT:
                    x_high(6)
                    x_high(7)
                if SQ_FROM <= t < SQ_FROM + E:
                    square_expert(t - SQ_FROM)
                if t == PIECE_STEPS[0]:
                    act.wait_ge(scaled, SKILLS + 1)
                if t in PIECES:
                    split_high(*PIECES[t])
                if hi_on_act(t):
                    high_part(t)
            act.wait_ge(tab_sk, 1)
            for k in range(TOP_K):
                gelu(SH_STEPS + k, k)
                if SH_STEPS + k in PIECES:
                    split_high(*PIECES[SH_STEPS + k])
                high_part(SH_STEPS + k)
            with act.Fori(1, B) as b:
                for k in range(TOP_K):
                    gelu(TOP_K * b + (SH_STEPS + k), k)

        @block.vector
        def _(dve):
            dve.wait_ge(cond_in, 16)
            nc.vector.tensor_reduce(neg_max[:, :], logits[:, :], AX.X, ALU.max, negate=True).then_inc(r_negmax, 1)
            dve.wait_ge(r_exp, 1)
            nc.vector.reciprocal(rsum[:, :], expsum[:, :]).then_inc(r_step, 1)
            dve.wait_ge(r_step, 1)
            nc.vector.tensor_scalar(probs[:, :], expv[:, :], rsum[:, 0:1], None, ALU.mult).then_inc(r_step, 1)
            dve.wait_ge(r_step, 2)
            nc.vector.max(top_v[:, :], probs[:, :]).then_inc(r_step, 1)
            dve.wait_ge(r_step, 3)
            nc.vector.max_index(top_i[:, :], top_v[:, :], probs[:, :]).then_inc(r_step, 1)
            nc.vector.tensor_tensor(pair[:, :], top_v[:, 0:1], top_v[:, 1:2], ALU.add).then_inc(r_step, 1)
            dve.wait_ge(r_step, 5)
            nc.vector.tensor_copy(route[:, TOP_K:], top_i[:, 0:TOP_K]).then_inc(r_step, 1)
            nc.vector.reciprocal(rpair[:, :], pair[:, :]).then_inc(r_step, 1)
            dve.wait_ge(r_step, 7)
            nc.vector.tensor_scalar(w_raw[:, :], top_v[:, 0:TOP_K], rpair[:, 0:1], None, ALU.mult).then_inc(r_step, 1)
            dve.wait_ge(r_step, 8)
            nc.vector.tensor_scalar(w_live[:, :], w_raw[:, :], 1.0 / NUM_MOE_LAYERS, None, ALU.mult).then_inc(r_step, 1)
            dve.wait_ge(r_step, 9)
            nc.vector.scalar_tensor_tensor(out=route[:, 0:TOP_K], in0=w_raw[:, :], scalar=1.0 - 1.0 / NUM_MOE_LAYERS,
                                           in1=w_live[:, :], op0=ALU.mult, op1=ALU.add).then_inc(r_step, 1)

            def scales(batch):
                a, b = BATCHES[batch]
                dve.wait_ge(n_red, batch + 1)
                nc.vector.tensor_scalar(e_half[:, a:b], n_all[:, a:b].bitcast(U32), EXP_SHIFT, None,
                                        ALU.logical_shift_right).then_inc(s_step, 1)
                dve.wait_ge(s_step, batch + 1)
                nc.vector.tensor_scalar(i_bits[:, a:b], e_half[:, a:b], ONE_EXP, INV_FIELD * ONE_EXP,
                                        ALU.mult, ALU.add)
                nc.vector.tensor_scalar(s_bits[:, a:b], e_half[:, a:b], -ONE_EXP, SCALE_FIELD * ONE_EXP,
                                        ALU.mult, ALU.add).then_inc(scaled, 1)
                dve.wait_ge(scaled, batch + 1)

            def x_low(j):
                dve.wait_ge(x_hi_ok, j + 1)
                nc.vector.scalar_tensor_tensor(out=x_lo[:, bass.ds(j * GN, GN)], in0=xT32[:, bass.ds(j * GN, GN)],
                                               scalar=sc[:, bass.ds(XC + j, 1)], in1=x_hi[:, bass.ds(j * GN, GN)],
                                               op0=ALU.mult, op1=ALU.subtract).then_inc(x_lo_ok, 1)

            def shared_tables(n, a, b):
                ix, sx = inv[:, XC + a:XC + b], sc[:, XC + a:XC + b]
                n_g = b - a
                nc.vector.tensor_scalar(gate_sc[:, a * C:b * C].rearrange("p (j c) -> p j c", c=C),
                                        ix.unsqueeze(2).broadcast_to([P, n_g, C]), inv[:, GC:GC + 1], None, ALU.mult)
                nc.vector.tensor_scalar(factor[:, a * C:b * C].rearrange("p (j c) -> p j c", c=C),
                                        sx.unsqueeze(2).broadcast_to([P, n_g, C]), HIDDEN_SHIFT, sc[:, GC:GC + 1],
                                        ALU.mult, ALU.mult).then_inc(tab_sh, 1)
                dve.wait_ge(tab_sh, n + 1)

            def output_table():
                nc.vector.tensor_scalar(tmp_g[:, 0, :], inv[:, XC:XC + G], inv[:, UC:UC + 1], 1.0 / HIDDEN_SHIFT,
                                        ALU.mult, ALU.mult).then_inc(t_step, 1)
                dve.wait_ge(t_step, 1)
                nc.vector.tensor_scalar(tmp_g[:, 1, :], tmp_g[:, 0, :], inv[:, DC:DC + 1], None, ALU.mult).then_inc(t_step, 1)
                dve.wait_ge(t_step, 2)
                nc.vector.tensor_tensor(sh_inv[:, :], tmp_g[:, 1, :], gate_sc[:, 0:SH_STEPS:C], ALU.mult).then_inc(tab_sh, 1)
                dve.wait_ge(tab_sh, 4)

            def hidden(t, kp, k4):
                dve.wait_ge(gelu_ready, t + 1)
                nc.vector.scalar_tensor_tensor(out=h32[:, k4, :], in0=gel[:, kp, :], scalar=factor[:, bass.ds(t, 1)],
                                               in1=u_ps[kp][:, :], op0=ALU.mult, op1=ALU.mult).then_inc(h_ready, 1)

            def high_part(t, k4):
                dve.wait_ge(h_ready, t + 1)
                nc.vector.tensor_copy(h_hi[:, k4, :], h32[:, k4, :]).then_inc(hi_ready, 1)

            def add_group(j, par):
                group = acc[:, bass.ds(j * GN, GN)]
                dve.wait_ge(group_done, j + 1)
                nc.vector.scalar_tensor_tensor(out=group, in0=out_ps[par][:, :], scalar=sh_inv[:, bass.ds(j, 1)], in1=group,
                                               op0=ALU.mult, op1=ALU.add).then_inc(added, 1)

            def add_row(b, k):
                row = acc[:, bass.ds(b * H, H)]
                dve.wait_ge(row_done, b + 1)
                nc.vector.scalar_tensor_tensor(out=row, in0=out_ps[k][:, 0:H], scalar=sk_inv[:, bass.ds(b, 1)], in1=row,
                                               op0=ALU.mult, op1=ALU.add).then_inc(half_added, 1)
                dve.wait_ge(half_added, b + 1)
                nc.vector.scalar_tensor_tensor(out=row, in0=out_ps[k][:, H:2 * H], scalar=sk_inv[:, bass.ds(b, 1)], in1=row,
                                               op0=ALU.mult, op1=ALU.add).then_inc(added, 1)

            def shared_low(q):
                col = (GC, UC, DC)[q]
                dve.wait_ge(sh_hi_ok, q + 1)
                nc.vector.scalar_tensor_tensor(out=wsh[:, 2 * q + 1, :], in0=wsh32[:, q * I:(q + 1) * I],
                                               scalar=sc[:, col:col + 1], in1=wsh[:, 2 * q, :],
                                               op0=ALU.mult, op1=ALU.subtract).then_inc(sh_lo_ok, 1)

            def skill_tables():
                ix, sx = inv[:, XC:XC + G], sc[:, XC:XC + G]
                nc.vector.tensor_scalar(tmp_k[:, 0, :], ix, inv[:, KC + 1:KC + 2], 1.0 / HIDDEN_SHIFT,
                                        ALU.mult, ALU.mult).then_inc(t_step, 1)
                nc.vector.tensor_scalar(tmp_k[:, 1, :], sx, HIDDEN_SHIFT, sc[:, KC:KC + 1], ALU.mult, ALU.mult).then_inc(t_step, 1)
                per_g = GR * TOP_K
                sk_gsc = gate_sc[:, SH_STEPS:].rearrange("p (j m) -> p j m", m=per_g)
                nc.vector.tensor_scalar(sk_gsc, ix.unsqueeze(2).broadcast_to([P, G, per_g]), inv[:, KC:KC + 1], None,
                                        ALU.mult).then_inc(t_step, 1)
                dve.wait_ge(t_step, 5)
                nc.vector.tensor_tensor(factor[:, SH_STEPS:].rearrange("p (j m) -> p j m", m=per_g),
                                        tmp_k[:, 1, :].unsqueeze(2).broadcast_to([P, G, per_g]),
                                        wexp[:, :, :].rearrange("p (j r) k -> p j (r k)", r=GR), ALU.mult)
                nc.vector.scalar_tensor_tensor(out=sk_inv[:, :].rearrange("p (j r) -> p j r", r=GR),
                                               in0=tmp_k[:, 0, :].unsqueeze(2).broadcast_to([P, G, GR]),
                                               scalar=inv[:, KC + 2:KC + 3], in1=sk_gsc[:, :, 0:GR],
                                               op0=ALU.mult, op1=ALU.mult).then_inc(tab_sk, 1)
                dve.wait_ge(tab_sk, 1)

            def split_low(t):
                q, c = PIECES[t]
                w, hi, lo = skill_piece(q, c)
                dve.wait_ge(sk_hi_ok, PIECE_STEPS.index(t) + 1)
                nc.vector.scalar_tensor_tensor(out=lo, in0=w, scalar=sc[:, KC + q:KC + q + 1], in1=hi,
                                               op0=ALU.mult, op1=ALU.subtract).then_inc(sk_lo_ok, 1)

            def spread_routing():
                dve.wait_ge(r_step, 10)
                dve.wait_ge(consts, 3)
                for q in range(2 * TOP_K):
                    nc.vector.tensor_scalar(spread[:, :, q], ident[0:B, 0:B], route[:, q:q + 1], None, ALU.mult).then_inc(r_spread, 1)

            dve.wait_ge(norms, 1)
            nc.vector.tensor_reduce(n_part[:, 0:XC + 1], norm_ps[:, 0:NRM_XR].rearrange("p (q c) -> p q c", q=2),
                                    AX.X, ALU.max).then_inc(n_max, 1)
            scales(FIRST)
            nc.vector.tensor_scalar(x_hi[:, 0:GN], xT32[:, 0:GN], sc[:, XC:XC + 1], None, ALU.mult).then_inc(x_hi_ok, 1)
            dve.wait_ge(norms, 2)
            nc.vector.tensor_reduce(n_part[:, UC:KC], norm_ud.rearrange("p (q c) -> p q c", q=2), AX.X, ALU.max).then_inc(n_max, 1)
            x_low(0)
            scales(UP_DOWN)
            shared_low(0)
            shared_low(1)
            shared_tables(0, 0, 1)
            dve.wait_ge(norms, 3)
            nc.vector.tensor_reduce(n_part[:, XC + 1:XC + XA], norm_xn.rearrange("p (j r) -> p j r", r=GR),
                                    AX.X, ALU.max).then_inc(n_max, 1)
            for t in range(SH_STEPS):
                j, c = t // C, t % C
                hidden(t, t % 2, t % 4)
                if not hi_on_act(t):
                    high_part(t, t % 4)
                if t == 0:
                    scales(X_NEXT)
                if t == 1:
                    shared_low(2)
                    x_low(1)
                if t == 2:
                    shared_tables(1, 1, XA)
                if t == 4:
                    spread_routing()
                    x_low(2)
                    dve.wait_ge(norms, 4)
                    nc.vector.tensor_reduce(n_part[:, XC + XA:UC], norm_ps[:, NRM_XR:NRM_SK].rearrange("p (j r) -> p j r", r=GR),
                                            AX.X, ALU.max).then_inc(n_max, 1)
                if t == 5:
                    x_low(3)
                    scales(X_REST)
                    shared_tables(2, XA, G)
                if t == 6:
                    output_table()
                if t == 7:
                    dve.wait_ge(r_routed, 1)
                    nc.vector.tensor_copy(wexp[:, :, :], routed[:, :, 0:TOP_K]).then_inc(r_table, 1)
                    nc.vector.tensor_scalar(eoff[:, :].rearrange("p (b k) -> p b k", b=B), routed[0:1, :, TOP_K:], float(P), None,
                                            ALU.mult).then_inc(r_table, 1)
                if t == 8:
                    x_low(4)
                if t == 9:
                    x_low(5)
                if t == NORMS_AT + 1:
                    x_low(6)
                if t == NORMS_AT + 2:
                    x_low(7)
                if c == C - 1 and j > 0:
                    if j == 1:
                        dve.wait_ge(xS_in, 16)
                    add_group(j - 1, (j - 1) % 2)
                if t == NORMS_AT:
                    dve.wait_ge(norms, 4 + E)
                    nc.vector.tensor_reduce(n_part[:, KC:NS], norm_ps[:, NRM_SK:NRM].rearrange("p (e q c) -> p q e c", e=E, q=3),
                                            AX.XY, ALU.max).then_inc(n_max, 1)
                if t == NORMS_AT + 1:
                    scales(SKILLS)
                if t == NORMS_AT + 2:
                    dve.wait_ge(r_table, 1)
                    skill_tables()
                if t - 1 in PIECES:
                    split_low(t - 1)
            for u in range(4):
                hidden(SH_STEPS + u, u % 2, u)
                if u == 2:
                    add_group(G - 1, 1)
                if not hi_on_act(SH_STEPS + u):
                    high_part(SH_STEPS + u, u)
                if SH_STEPS + u - 1 in PIECES:
                    split_low(SH_STEPS + u - 1)
            with dve.Fori(0, B // 2 - 1) as i:
                for v in range(4):
                    hidden(4 * i + (SH_STEPS + 4 + v), v % 2, v)
                    if v % 2 == 0:
                        add_row(2 * i + v // 2, v // 2)
                    high_part(4 * i + (SH_STEPS + 4 + v), v)
            dve.wait_ge(hi_ready, STEPS - ACT_HIGHS)
            nc.vector.tensor_tensor(h_lo[:, 3, :], h32[:, 3, :], h_hi[:, 3, :], ALU.subtract).then_inc(last_lo, 1)
            for v in range(2):
                add_row(B - 2 + v, v)

        @block.tensor
        def _(pe):
            def norm_columns(out, sq):
                for c in range(out.shape[1]):
                    last = nc.tensor.matmul(out[:, c:c + 1], sq[:, c * P:(c + 1) * P], ones_col[:, :], start=True, stop=True)
                return last

            def norms_expert(e):
                pe.wait_ge(sq_act, 7 + e)
                m, o = 3 * C, (e % 2) * W
                norm_columns(norm_ps[:, NRM_SK + e * m:NRM_SK + (e + 1) * m], sq_w[:, o:o + W]).then_inc(norms, 1)

            def gate_up_shared(t, j, c, kp, first=False):
                if not isinstance(t, int) or t >= 2:
                    pe.wait_ge(h_ready, t - 1)
                xh, xl = x_hi[:, bass.ds(j * GN, GN)], x_lo[:, bass.ds(j * GN, GN)]
                for out, m in ((g_ps[kp], GATE), (u_ps[kp], UP)):
                    w_hi, w_lo = wsh[:, m, c * P:(c + 1) * P], wsh[:, m + 1, c * P:(c + 1) * P]
                    if first:
                        if m == GATE:
                            pe.wait_ge(x_hi_ok, 1)
                        pe.wait_ge(sh_hi_ok, m // 2 + 1)
                    nc.tensor.matmul(out[:, :], w_hi, xh, start=True, stop=False)
                    if first and m == GATE:
                        pe.wait_ge(x_lo_ok, 1)
                    nc.tensor.matmul(out[:, :], w_hi, xl, start=False, stop=False)
                    if first:
                        pe.wait_ge(sh_lo_ok, m // 2 + 1)
                    last = nc.tensor.matmul(out[:, :], w_lo, xh, start=False, stop=True)
                last.then_inc(gu_ready, 1)

            def down_shared(t, par, c, k4):
                pe.wait_ge(lo_ready, t + 1)
                w_hi, w_lo = wsh[:, DOWN, c * P:(c + 1) * P], wsh[:, DOWN + 1, c * P:(c + 1) * P]
                for r in range(GR):
                    out, rows = out_ps[par][:, r * H:(r + 1) * H], slice(r * S, (r + 1) * S)
                    hi, lo = h_hi[:, k4, rows], h_lo[:, k4, rows]
                    nc.tensor.matmul(out, hi, w_hi, start=(c == 0 and r == 0), stop=False, skip_group_check=True)
                    nc.tensor.matmul(out, hi, w_lo, start=False, stop=False, skip_group_check=True)
                    last = nc.tensor.matmul(out, lo, w_hi, start=False, stop=(c == C - 1), skip_group_check=True)
                if c == C - 1:
                    last.then_inc(group_done, 1)

            def experts(first, n):
                _, e = nc.values_load_multi_w_load_instructions(
                    eoff[0:1, bass.ds(first, n)], engines=[pe.engine], min_val=0, max_val=(E - 1) * P,
                    skip_runtime_bounds_check_because="the indices of the largest of E probabilities are 0 to E - 1")
                return e

            def gate_up_skill(u, b, k, e):
                xh, xl = x_hi[:, bass.ds(b * S, S)], x_lo[:, bass.ds(b * S, S)]
                for out, m in ((g_ps[k], 0), (u_ps[k], 2)):
                    w_hi, w_lo = ([w[:, bass.ds(e, P)] for w in wsk_gu[n]] for n in (m, m + 1))
                    if m == 0:
                        pe.lower_ap(xh)
                        pe.lower_ap(xl)
                    for ap in w_hi + w_lo:
                        pe.lower_ap(ap, for_matmul_weights=True)
                    if m == 0:
                        pe.wait_ge(h_ready, u + (SH_STEPS - 1))
                    for c in range(C):
                        cols = out[:, c * S:(c + 1) * S]
                        nc.tensor.matmul(cols, w_hi[c], xh, start=True, stop=False)
                        nc.tensor.matmul(cols, w_hi[c], xl, start=False, stop=False)
                        last = nc.tensor.matmul(cols, w_lo[c], xh, start=False, stop=True)
                last.then_inc(gu_ready, 1)

            def down_weights(e):
                pairs = [w[:, 0:2, bass.ds(e, P)] for w in wsk_down]
                for ap in pairs:
                    pe.lower_ap(ap)
                return pairs

            def wait_low(u):
                pe.wait_ge(lo_ready, u + (SH_STEPS + 1))

            def down_skill(k, par, k4, w_dn):
                for c in range(C):
                    first, final = k == 0 and c == 0, k == TOP_K - 1 and c == C - 1
                    w_pair = w_dn[c]
                    hi, lo = h_hi[:, k4, c * S:(c + 1) * S], h_lo[:, k4, c * S:(c + 1) * S]
                    nc.tensor.matmul(out_ps[par][:, 0:2 * H], hi, w_pair, start=first, stop=final, skip_group_check=True)
                    last = nc.tensor.matmul(out_ps[par][:, 0:H], lo, w_pair[:, 0, :], start=False, stop=final,
                                            skip_group_check=True)
                if k == TOP_K - 1:
                    last.then_inc(row_done, 1)

            def keep_warm(n):
                for _ in range(n):
                    nc.tensor.matmul(g_ps[0][:, :], zeros[:, 0:P], zeros[:, :], start=True, stop=True)

            pe.wait_ge(zeros_ok, 1)
            keep_warm(WARM_BEFORE)
            pe.wait_ge(consts, 3)
            pe.wait_ge(sq_act, 1)
            norm_columns(norm_ps[:, NRM_X0:NRM_XR], sq_x[:, 0:GN])
            keep_warm(WARM_SPLIT)
            pe.wait_ge(sq_act, 2)
            norm_columns(norm_ps[:, 0:NRM_X0], sq_w[:, 0:I]).then_inc(norms, 1)
            pe.wait_ge(sq_act, 3)
            norm_columns(norm_ud, sq_w[:, I:W]).then_inc(norms, 1)
            keep_warm(WARM_AFTER)
            for c in range(C):
                gate_up_shared(c, 0, c, c % 2, first=(c == 0))
                if c == 0:
                    pe.wait_ge(sq_act, 4)
                    norm_columns(norm_xn, sq_x[:, GN:XA * GN]).then_inc(norms, 1)
                if c == LAG:
                    pe.wait_ge(sh_lo_ok, 3)
                    down_shared(0, 0, 0, 0)

            def group(j, par, norms_from=None):
                pe.wait_ge(x_lo_ok, j + 1)
                for c in range(C):
                    t = j * C + c
                    gate_up_shared(t, j, c, c % 2)
                    down_shared(t - LAG, par if c >= LAG else 1 - par, (c - LAG) % C, (c - LAG) % 4)
                    if isinstance(j, int) and t == C:
                        pe.wait_ge(sq_act, 6)
                        norm_columns(norm_ps[:, NRM_XR:NRM_SK], sq_x[:, XA * GN:]).then_inc(norms, 1)
                    if isinstance(j, int) and t == C + 2:
                        pe.wait_ge(r_spread, 2 * TOP_K)
                        nc.tensor.matmul(route_bc, ones32[:, :], spread[:, :, :].rearrange("p b q -> p (b q)"),
                                         start=True, stop=True).then_inc(r_routed, 1)
                    if norms_from is not None and 0 <= t - norms_from < E:
                        norms_expert(t - norms_from)

            for j in range(1, SPLIT_FROM):
                group(j, j % 2, SQ_FROM + 1)
            with pe.Fori(0, (G - SPLIT_FROM) // 2) as n:
                for par in range(2):
                    group(2 * n + (SPLIT_FROM + par), par)
            pe.wait_ge(r_table, 2)
            e = experts(0, 2 * TOP_K)
            pe.wait_ge(sk_lo_ok, SK_GU)
            for u in range(LAG):
                gate_up_skill(u, u // TOP_K, u % TOP_K, e[u])
                down_shared(SH_STEPS - LAG + u, 1, C - LAG + u, C - LAG + u)
            gate_up_skill(LAG, LAG // TOP_K, LAG % TOP_K, e[LAG])
            w_dn = down_weights(e[0])
            pe.wait_ge(sk_lo_ok, 3 * C)
            wait_low(0)
            down_skill(0, 0, 0, w_dn)
            with pe.Fori(0, B // 2 - 1) as i:
                e = experts(4 * i + 1, LAG + 4)
                for v in range(4):
                    gate_up_skill(4 * i + (4 + v), 2 * i + (2 + v // TOP_K), v % TOP_K, e[LAG + v])
                    w_dn = down_weights(e[v])
                    wait_low(4 * i + (1 + v))
                    down_skill((1 + v) % TOP_K, (1 + v) // TOP_K % 2, (1 + v) % 4, w_dn)
            e = experts(TOP_K * B - LAG, LAG)
            wait_low(TOP_K * B - LAG)
            down_skill(1, 0, 1, down_weights(e[0]))
            out = out_ps[1]
            for k in range(TOP_K):
                w_dn = down_weights(e[1 + k])
                pe.wait_ge(hi_ready, STEPS - ACT_HIGHS - 1 + k)
                for c in range(C):
                    nc.tensor.matmul(out[:, 0:2 * H], h_hi[:, 2 + k, c * S:(c + 1) * S], w_dn[c], start=(k == 0 and c == 0),
                                     stop=False, skip_group_check=True)
                pe.wait_ge(*((lo_ready, STEPS - 1), (last_lo, 1))[k])
                for c in range(C):
                    last = nc.tensor.matmul(out[:, 0:H], h_lo[:, 2 + k, c * S:(c + 1) * S], w_dn[c][:, 0, :], start=False,
                                            stop=(k == TOP_K - 1 and c == C - 1), skip_group_check=True)
            last.then_inc(row_done, 1)


def kernel(x, cond_8, L0_cond_skill_gate, L0_cond_skill_up, L0_cond_skill_down, L0_cond_shared_gate,
           L0_cond_shared_up, L0_cond_shared_down):
    import numpy as np
    import concourse.bacc as bacc
    from concourse.bass_utils import run_bass_kernel_spmd

    x, cond = np.asarray(x), np.ascontiguousarray(cond_8)
    sg, su, sd = np.asarray(L0_cond_skill_gate), np.asarray(L0_cond_skill_up), np.asarray(L0_cond_skill_down)
    hg, hu, hd = np.asarray(L0_cond_shared_gate), np.asarray(L0_cond_shared_up), np.asarray(L0_cond_shared_down)
    B, S, H = x.shape
    E, _, I = sg.shape
    C = I // 128
    xT = np.ascontiguousarray(x.transpose(2, 0, 1).reshape(H, B * S))
    skills = np.ascontiguousarray(np.concatenate(
        [sg.transpose(1, 0, 2), su.transpose(1, 0, 2),
         sd.reshape(E, C, 128, H).transpose(2, 0, 1, 3).reshape(128, E, C * H)], axis=2).reshape(128, -1))
    shared = np.ascontiguousarray(np.concatenate([hg, hu, hd.reshape(C, 128, H).transpose(1, 0, 2).reshape(128, C * H)], axis=1))
    xS = np.ascontiguousarray(x.transpose(1, 0, 2).reshape(S, B * H))
    arrays = {"xT": xT, "xS": xS, "cond": cond, "skills": skills, "shared": shared}

    nc = bacc.Bacc("TRN2", target_bir_lowering=False, num_devices=1)
    aps = {n: nc.dram_tensor(n, a.shape, mybir.dt.from_np(a.dtype), kind="ExternalInput").ap() for n, a in arrays.items()}
    outS = nc.dram_tensor("outS", xS.shape, F32, kind="ExternalOutput").ap()
    build(nc, aps["xT"], aps["xS"], aps["cond"], aps["skills"], aps["shared"], outS)
    got = run_bass_kernel_spmd(nc, [arrays], core_ids=[0]).results[0]["outS"]
    return np.ascontiguousarray(got.reshape(S, B, H).transpose(1, 0, 2))
```
